# Optimizing a Trainium2 kernel written in Bass

```python
import numpy as np
import jax
import jax.numpy as jnp

def _softmax(x, axis=-1):
    return jax.nn.softmax(x, axis=axis)
def _gelu(x):
    return jax.nn.gelu(x, approximate=True)
def _silu(x):
    return jax.nn.silu(x)
def _sigmoid(x):
    return jax.nn.sigmoid(x)
def _layernorm(x, axis=-1, eps=1e-5):
    m = jnp.mean(x, axis=axis, keepdims=True)
    v = jnp.var(x, axis=axis, keepdims=True)
    return (x - m) / jnp.sqrt(v + eps)
def _scatter_add(tgt, idx, src, axis=0):
    return tgt.at[idx].add(src)
def _segment_sum(src, seg, n):
    return jax.ops.segment_sum(src, seg, n)

kernel_name = 'mk_conv_preact_d2_conv_nchw64_d5a6e7'

def setup_inputs(seed: int = 0):
    np.random.seed(seed)
    _w = jnp.asarray
    def _rec_inputs():
        import jax
        import jax.numpy as jnp
        _gk = jax.random.key(seed)
        x = -0.000125 + 0.9999 * jax.random.normal(jax.random.fold_in(_gk, 1), (8, 64, 256, 256), jnp.float32)
        return x
    x = _rec_inputs()
    def _L0_conv_setup():
        import jax, jax.numpy as jnp
        import numpy as np
        S = 1.0 / np.sqrt(2.0).astype(np.float32)

        def _dwt_axis(x, axis):
            x = jnp.moveaxis(x, axis, -1)
            n = x.shape[-1]
            xp = x.reshape(x.shape[:-1] + (n // 2, 2))
            lo = (xp[..., 0] + xp[..., 1]) * S
            hi = (xp[..., 0] - xp[..., 1]) * S
            return (jnp.moveaxis(lo, -1, axis), jnp.moveaxis(hi, -1, axis))

        def _idwt_axis(lo, hi, axis, orig_len):
            lo = jnp.moveaxis(lo, axis, -1)
            hi = jnp.moveaxis(hi, axis, -1)
            even = (lo + hi) * S
            odd = (lo - hi) * S
            rec = jnp.stack([even, odd], axis=-1).reshape(lo.shape[:-1] + (2 * lo.shape[-1],))
            rec = rec[..., :orig_len]
            return jnp.moveaxis(rec, -1, axis)

        def _mix(sub, W, b):
            return jnp.einsum('oc,bchw->bohw', W, sub) + b[None, :, None, None]
        key = jax.random.key(seed)
        B, C, H, W = (8, 64, 256, 256)
        ks = jax.random.split(key, 9)
        scale = 1.0 / C
        inp = {'x': jax.random.normal(ks[0], (B, C, H, W), dtype=jnp.float32)}
        for i, name in enumerate(['LL', 'LH', 'HL', 'HH']):
            inp[f'w_{name}'] = jax.random.uniform(ks[1 + i], (C, C), jnp.float32, -scale, scale)
            inp[f'b_{name}'] = jnp.zeros((C,), jnp.float32)
        return inp
    _L0_conv_all = _L0_conv_setup()
    _L0_conv_in = {k: v for k, v in _L0_conv_all.items() if k in ('w_LL', 'b_LL', 'w_LH', 'b_LH', 'w_HL', 'b_HL', 'w_HH', 'b_HH', )}
    del _L0_conv_all

    def _L1_conv_setup():
        import jax, jax.numpy as jnp
        import numpy as np
        MODES1 = 32
        MODES2 = 32

        def _dct1_last(x):
            ext = jnp.concatenate([x, x[..., -2:0:-1]], axis=-1)
            return jnp.fft.rfft(ext, axis=-1).real.astype(x.dtype)

        def _dct1_2d(x):
            x = _dct1_last(x)
            x = jnp.swapaxes(x, -1, -2)
            x = _dct1_last(x)
            return jnp.swapaxes(x, -1, -2)
        key = jax.random.key(seed)
        k1, k2, k3 = jax.random.split(key, 3)
        B, Cin, Cout, H, W = (8, 64, 64, 256, 256)
        scale = 1.0 / (Cin * Cout)
        x = jax.random.normal(k1, (B, Cin, H, W), dtype=jnp.float32)
        weights1 = scale * jax.random.uniform(k2, (Cin, Cout, MODES1, MODES2), dtype=jnp.float32)
        weights2 = scale * jax.random.uniform(k3, (Cin, Cout, MODES1, MODES2), dtype=jnp.float32)
        return {'x': x, 'weights1': weights1, 'weights2': weights2}
    _L1_conv_all = _L1_conv_setup()
    _L1_conv_in = {k: v for k, v in _L1_conv_all.items() if k in ('weights1', 'weights2', )}
    del _L1_conv_all

    return {
        "x": x,
        "L0_conv_w_LL": _L0_conv_in["w_LL"],
        "L0_conv_b_LL": _L0_conv_in["b_LL"],
        "L0_conv_w_LH": _L0_conv_in["w_LH"],
        "L0_conv_b_LH": _L0_conv_in["b_LH"],
        "L0_conv_w_HL": _L0_conv_in["w_HL"],
        "L0_conv_b_HL": _L0_conv_in["b_HL"],
        "L0_conv_w_HH": _L0_conv_in["w_HH"],
        "L0_conv_b_HH": _L0_conv_in["b_HH"],
        "L1_conv_weights1": _L1_conv_in["weights1"],
        "L1_conv_weights2": _L1_conv_in["weights2"],
    }

def reference(x, L0_conv_w_LL, L0_conv_b_LL, L0_conv_w_LH, L0_conv_b_LH, L0_conv_w_HL, L0_conv_b_HL, L0_conv_w_HH, L0_conv_b_HH, L1_conv_weights1, L1_conv_weights2):
    import jax
    import jax.numpy as jnp
    def _L0_conv_ref(x, w_LL, b_LL, w_LH, b_LH, w_HL, b_HL, w_HH, b_HH):
        import jax, jax.numpy as jnp
        import numpy as np
        S = 1.0 / np.sqrt(2.0).astype(np.float32)

        def _dwt_axis(x, axis):
            x = jnp.moveaxis(x, axis, -1)
            n = x.shape[-1]
            xp = x.reshape(x.shape[:-1] + (n // 2, 2))
            lo = (xp[..., 0] + xp[..., 1]) * S
            hi = (xp[..., 0] - xp[..., 1]) * S
            return (jnp.moveaxis(lo, -1, axis), jnp.moveaxis(hi, -1, axis))

        def _idwt_axis(lo, hi, axis, orig_len):
            lo = jnp.moveaxis(lo, axis, -1)
            hi = jnp.moveaxis(hi, axis, -1)
            even = (lo + hi) * S
            odd = (lo - hi) * S
            rec = jnp.stack([even, odd], axis=-1).reshape(lo.shape[:-1] + (2 * lo.shape[-1],))
            rec = rec[..., :orig_len]
            return jnp.moveaxis(rec, -1, axis)

        def _mix(sub, W, b):
            return jnp.einsum('oc,bchw->bohw', W, sub) + b[None, :, None, None]
        B, C, H, W = x.shape
        Lw, Hw = _dwt_axis(x, -1)
        LL, LH = _dwt_axis(Lw, -2)
        HL, HH = _dwt_axis(Hw, -2)
        LL = _mix(LL, w_LL, b_LL)
        LH = _mix(LH, w_LH, b_LH)
        HL = _mix(HL, w_HL, b_HL)
        HH = _mix(HH, w_HH, b_HH)
        Lw_r = _idwt_axis(LL, LH, -2, H)
        Hw_r = _idwt_axis(HL, HH, -2, H)
        return _idwt_axis(Lw_r, Hw_r, -1, W)

    def _L1_conv_ref(x, weights1, weights2):
        import jax, jax.numpy as jnp
        import numpy as np
        MODES1 = 32
        MODES2 = 32

        def _dct1_last(x):
            ext = jnp.concatenate([x, x[..., -2:0:-1]], axis=-1)
            return jnp.fft.rfft(ext, axis=-1).real.astype(x.dtype)

        def _dct1_2d(x):
            x = _dct1_last(x)
            x = jnp.swapaxes(x, -1, -2)
            x = _dct1_last(x)
            return jnp.swapaxes(x, -1, -2)
        B, Cin, H, W = x.shape
        Cout = weights1.shape[1]
        Wh = W // 2 + 1
        m1, m2 = (MODES1, MODES2)
        x_dct = _dct1_2d(x)
        low = jnp.einsum('bixy,ioxy->boxy', x_dct[:, :, :m1, :m2], weights1)
        high = jnp.einsum('bixy,ioxy->boxy', x_dct[:, :, -m1:, :m2], weights2)
        out_ft = jnp.zeros((B, Cout, H, Wh), dtype=x.dtype)
        out_ft = out_ft.at[:, :, :m1, :m2].set(low)
        out_ft = out_ft.at[:, :, H - m1:, :m2].set(high)
        out_full = jnp.pad(out_ft, ((0, 0), (0, 0), (0, 0), (0, W - Wh)))
        return _dct1_2d(out_full)

    def _gn(v, G=32, eps=1e-5):
        B_, C_, H_, W_ = v.shape
        g = v.reshape(B_, G, C_ // G, H_, W_)
        m = jnp.mean(g, axis=(2, 3, 4), keepdims=True)
        s = jnp.var(g, axis=(2, 3, 4), keepdims=True)
        return ((g - m) / jnp.sqrt(s + eps)).reshape(v.shape)

    def _ln_c(v, eps=1e-6):
        m = jnp.mean(v, axis=1, keepdims=True)
        s = jnp.var(v, axis=1, keepdims=True)
        return (v - m) / jnp.sqrt(s + eps)

    def _ln_t(v, eps=1e-5):
        m = jnp.mean(v, axis=-1, keepdims=True)
        s = jnp.var(v, axis=-1, keepdims=True)
        return (v - m) / jnp.sqrt(s + eps)

    def _to_tokens(v):
        B_, C_, H_, W_ = v.shape
        return v.reshape(B_, C_, H_ * W_).transpose(0, 2, 1)
    def _from_tokens(t, like):
        B_, C_, H_, W_ = like.shape
        return t.transpose(0, 2, 1).reshape(B_, C_, H_, W_)

    x = x + _L0_conv_ref(_gn(x), L0_conv_w_LL, L0_conv_b_LL, L0_conv_w_LH, L0_conv_b_LH, L0_conv_w_HL, L0_conv_b_HL, L0_conv_w_HH, L0_conv_b_HH)
    x = x + _L1_conv_ref(_gn(x), L1_conv_weights1, L1_conv_weights2)
    return x


_drawn_inputs = setup_inputs


def setup_inputs(seed=0):
    import zlib

    import numpy as np

    out = dict(_drawn_inputs(seed))
    spreads = {'L0_conv_b_LL': (0.0, 0.1),
     'L0_conv_b_LH': (0.0, 0.1),
     'L0_conv_b_HL': (0.0, 0.8),
     'L0_conv_b_HH': (0.0, 0.8)}
    factors = {'L0_conv_w_HL': 8.0, 'L0_conv_w_HH': 8.0}
    for name, (base, spread) in spreads.items():
        noise = np.random.default_rng([zlib.crc32(name.encode()), seed]).standard_normal(out[name].shape)
        drawn = base * np.exp(spread * noise) if base else spread * noise
        out[name] = jnp.asarray(drawn.astype(out[name].dtype))
    for name, factor in factors.items():
        out[name] = (out[name] * factor).astype(out[name].dtype)
    return out
```

```python
from contextlib import ExitStack

import concourse.bass as bass
from concourse import mybir
import numpy as np

F32 = mybir.dt.float32
ALU = mybir.AluOpType
ACT = mybir.ActivationFunctionType
ds = bass.ds

P = 128
B, C, H, W = 8, 64, 256, 256
MODES = 32
HP, WP = H // 2, W // 2
K2 = 2 * MODES
CHUNK = 8
CHUNKS = HP // CHUNK
PAIRS = CHUNKS // 2
GROUP = 4
GROUPS = HP // GROUP
GCOLS = GROUP * WP
QUADS = MODES // 4
EPS = 1e-5
HPITCH = P * W + 1024
OCT = C // 8

TABLE = {}
_at = 0
for _name, _width in (("ident", P), ("gavg", P), ("half", P), ("dw", 2 * MODES), ("dh", 2 * K2),
                      ("ch", 2 * HP), ("cw", 2 * WP), ("sign", 2), ("eps", 2), ("power", 2)):
    TABLE[_name] = (_at, _at + _width)
    _at += _width
TABLE_COLS = _at


def table_of_constants():
    t = np.zeros((P, TABLE_COLS), np.float64)

    def put(name, a, rows=slice(0, P)):
        lo, hi = TABLE[name]
        t[rows, lo:hi] = a.reshape(a.shape[0], -1)

    part = np.arange(P)
    put("ident", np.eye(P))
    group = (part % C) // 2
    put("gavg", (group[:, None] == group[None, :]) / 4.0)
    put("half", 0.5 * np.eye(P))
    rows = np.concatenate([np.arange(MODES), H - MODES + np.arange(MODES)])
    space = np.arange(H)
    cosines = np.cos(np.pi * ((rows[:, None] * space[None, :]) % (2 * (H - 1))) / (H - 1))
    ends_space = np.where((space == 0) | (space == H - 1), 1.0, 2.0)
    ends_rows = np.where((rows == 0) | (rows == H - 1), 1.0, 2.0)
    forward = cosines * ends_space[None, :]
    inverse = cosines * ends_rows[:, None]
    even, odd = forward[:MODES, 0::2], forward[:MODES, 1::2]
    put("dw", np.stack([even + odd, even - odd]).transpose(2, 0, 1))
    put("dh", np.stack([forward[:, 0::2], forward[:, 1::2]]).transpose(2, 0, 1))
    ch = np.stack([inverse[:, 0::2], inverse[:, 1::2]], axis=1)
    put("ch", np.concatenate([ch, ch]))
    even, odd = inverse[:MODES, 0::2], inverse[:MODES, 1::2]
    put("cw", np.stack([(even + odd) / 2, (even - odd) / 2], axis=1), slice(0, MODES))
    upper = np.where(part < C, 1.0, -1.0)
    put("sign", np.stack([upper, -upper], axis=1))
    put("eps", np.tile([[4 * EPS, EPS]], (P, 1)))
    put("power", np.full((P, 2), -0.5))
    return t.astype(np.float32)


def stage_one(nc, tab, x, mix_t, biases, x1_scr, spec_scr):
    with ExitStack() as ctx:
        def sb(name, shape):
            return ctx.enter_context(nc.sbuf_tensor(name, shape, F32))

        def sem(name):
            return ctx.enter_context(nc.semaphore(name))

        raw = [sb(f"raw{i}", [P, CHUNK, 2, WP]) for i in range(2)]
        lh = sb("lh", [P, CHUNKS * 2 * 2 * GCOLS])
        x1 = [sb(f"x1_{i}", [P, CHUNK, 2, WP]) for i in range(2)]
        x1t = [sb(f"x1t{i}", [P, 4, P]) for i in range(2)]
        aw = sb("aw", [P, HP * MODES])
        awt = [sb(f"awt{i}", [P, 4, P]) for i in range(2)]
        spec = sb("spec", [C, 2, MODES, MODES])
        wraw = sb("wraw", [P, 4, C])
        mt = sb("mt", [P, 2, P])
        wlh = sb("wlh", [P, 2, P])
        braw = sb("braw", [P, 4])
        bconst = sb("bconst", [P, 2])
        bias = sb("bias", [P, 2])
        st_x = sb("st_x", [P, 2, GROUPS * 6])
        st_x1 = sb("st_x1", [P, 2, GROUPS * 6])
        agg = sb("agg", [P, 2, 2, 2])
        vec = sb("vec", [P, 2, 2])
        gst = sb("gst", [P, 2, 2])
        sm = sb("sm", [P, 2, 2])
        var = sb("var", [P, 2])
        rstd = sb("rstd", [P, 2])
        rm = sb("rm", [P, 2])

        ps_mix = [ctx.enter_context(nc.psum_tensor(f"ps_mix{i}", [P, 512], F32)) for i in range(4)]
        ps_t = [ctx.enter_context(nc.psum_tensor(f"ps_t{i}", [P, 512], F32)) for i in range(2)]
        ps_aw = ctx.enter_context(nc.psum_tensor("ps_aw", [P, 512], F32))
        ps_st = ctx.enter_context(nc.psum_tensor("ps_st", [P, 512], F32))

        params_in = sem("params_in")
        mats_ready = sem("mats_ready")
        loaded = [sem(f"loaded{i}") for i in range(2)]
        low_done = sem("low_done")
        high_done = sem("high_done")
        vec_ready = sem("vec_ready")
        group_sum = sem("group_sum")
        var_ready = sem("var_ready")
        pow_done = sem("pow_done")
        rm_ready = sem("rm_ready")
        mean_mix = sem("mean_mix")
        wlh_ready = sem("wlh_ready")
        bias_ready = sem("bias_ready")
        mixed = sem("mixed")
        x1_ready = sem("x1_ready")
        x_stats = sem("x_stats")
        x1_stats = [sem(f"x1_stats{i}") for i in range(2)]
        stored = [sem(f"stored{i}") for i in range(2)]
        turned = sem("turned")
        x1t_ready = sem("x1t_ready")
        w_done = sem("w_done")
        aw_ready = sem("aw_ready")
        aw_turned = sem("aw_turned")
        awt_ready = sem("awt_ready")
        h_done = sem("h_done")
        spec_read = sem("spec_read")
        spec_ready = sem("spec_ready")
        spec_stored = sem("spec_stored")
        chain = sem("chain")

        def lh_cols(c, g, s, cols=GCOLS):
            return ds(c * (4 * GCOLS) + (g * 2 + s) * GCOLS, cols)

        block = ctx.enter_context(nc.Block())

        @block.sync
        def _(sp):
            for buf in range(2):
                sp.sem_inc(stored[buf], 16)
            for half in range(2):
                sp.dma_start(wraw[C * half:C * half + C], mix_t).then_inc(params_in, 16)
                sp.dma_start(braw[C * half:C * half + C], biases).then_inc(params_in, 16)

            def load(row, buf):
                sp.dma_start(raw[buf][:, :, :, :].rearrange("p r j w -> p (r j w)"), x[row, :, :].rearrange("a p m -> p (a m)")).then_inc(loaded[buf], 16)

            for buf in range(2):
                load(ds(buf, 1), buf)
            with sp.Fori(1, PAIRS) as k:
                for buf in range(2):
                    sp.wait_ge(low_done, 2 * k + buf - 1)
                    sp.wait_ge(high_done, 2 * k + buf - 1)
                    load(ds(2 * k + buf, 1), buf)

            def store(row, count, buf):
                sp.wait_ge(x1_ready, count)
                sp.dma_start(x1_scr[row, 0:P * W].rearrange("r (p w) -> p r w", w=W),
                             x1[buf][:, :, :, :].rearrange("p r j w -> p r (j w)")).then_inc(stored[buf], 16)

            with sp.Fori(0, PAIRS * (B - 1)) as k:
                for buf in range(2):
                    sp.wait_ge(low_done, 2 * k + CHUNKS + buf - 1)
                    sp.wait_ge(high_done, 2 * k + CHUNKS + buf - 1)
                    load(ds(2 * k + CHUNKS + buf, 1), buf)
                for buf in range(2):
                    store(ds((2 * k + buf) * CHUNK, CHUNK), 4 * k + 2 * buf + 2, buf)
            with sp.Fori(PAIRS * (B - 1), PAIRS * B) as k:
                for buf in range(2):
                    store(ds((2 * k + buf) * CHUNK, CHUNK), 4 * k + 2 * buf + 2, buf)
            for buf in range(2):
                sp.wait_ge(stored[buf], 16 * (PAIRS * B) + 16)

        @block.gpsimd
        def _(pool):
            def high(c, buf):
                v = raw[buf][:, :, :, :]
                for g in range(2):
                    out = lh[:, lh_cols(c, g, 1)].rearrange("p (r w) -> p r w", w=WP)
                    rows = slice(GROUP * g, GROUP * g + GROUP)
                    ins = pool.tensor_tensor(out, v[:, rows, 0, :], v[:, rows, 1, :], ALU.subtract)
                ins.then_inc(high_done, 1)

            def power(step):
                pool.wait_ge(var_ready, step)
                pool.tensor_tensor(rstd[:, :], var[:, :], tab("power"), ALU.pow).then_inc(pow_done, 1)

            pool.wait_ge(mats_ready, 1)
            with pool.Fori(0, PAIRS) as k:
                for buf in range(2):
                    pool.wait_ge(loaded[buf], 16 * k + 16)
                    high(2 * k + buf, buf)
            power(1)
            with pool.Fori(0, B - 1) as b:
                with pool.Fori(0, PAIRS) as k:
                    for buf in range(2):
                        pool.wait_ge(mixed, b * GROUPS + 4 * k + 2 * buf + 2)
                        pool.wait_ge(loaded[buf], (b * PAIRS + PAIRS + k) * 16 + 16)
                        high(2 * k + buf, buf)
                power(b + 2)
            power(B + 1)

        @block.vector
        def _(dve):
            links = [0]

            def link(ins):
                links[0] += 1
                ins.then_inc(chain, 1)
                dve.wait_ge(chain, links[0] if base[0] is None else base[0] + links[0])

            base = [None]

            for buf in range(2):
                dve.sem_inc(x1_stats[buf], 1)
            for half in range(2):
                dve.memset(st_x1[:, half, :], 1.0).then_inc(chain, 1)
            links[0] = 2
            dve.wait_ge(chain, 2)
            dve.wait_ge(params_in, 16 * 4)
            for s in range(2):
                lo, hi = wraw[:, 2 * s, :], wraw[:, 2 * s + 1, :]
                for i in range(2):
                    link(dve.scalar_tensor_tensor(mt[:, s, C * i:C * i + C], hi, tab("sign")[:, i:i + 1], lo,
                                                  ALU.mult, ALU.add))
                link(dve.scalar_tensor_tensor(bconst[:, s:s + 1], braw[:, 2 * s + 1:2 * s + 2],
                                              tab("sign")[:, 0:1], braw[:, 2 * s:2 * s + 1], ALU.mult, ALU.add))
            link(dve.tensor_scalar(mt[:, :, :], mt[:, :, :], 0.5, None, ALU.mult))
            link(dve.tensor_scalar(bconst[:, :], bconst[:, :], 0.5, None, ALU.mult))
            link(dve.tensor_copy(bias[:, 1:2], bconst[:, 1:2]))
            dve.sem_inc(mats_ready, 1)
            PROLOGUE = links[0]

            def low(c, buf):
                v = raw[buf][:, :, :, :]
                for g in range(2):
                    out = lh[:, lh_cols(c, g, 0)].rearrange("p (r w) -> p r w", w=WP)
                    rows = slice(GROUP * g, GROUP * g + GROUP)
                    ins = dve.tensor_tensor(out, v[:, rows, 0, :], v[:, rows, 1, :], ALU.add)
                ins.then_inc(low_done, 1)

            def stats_x(c, n):
                dve.wait_ge(low_done, n)
                dve.wait_ge(high_done, n)
                for g in range(2):
                    for s in range(2):
                        ins = dve.bn_stats(st_x[:, s, ds(c * 12 + g * 6, 6)], lh[:, lh_cols(c, g, s)])
                ins.then_inc(x_stats, 1)

            def stats_x1(k, buf, count):
                dve.wait_ge(x1_ready, count)
                for g in range(2):
                    for s in range(2):
                        ins = dve.bn_stats(st_x1[:, s, ds(k * 24 + buf * 12 + g * 6, 6)],
                                           x1[buf][:, GROUP * g:GROUP * g + GROUP, s, :])
                ins.then_inc(x1_stats[buf], 1)

            STEPS = 10

            def stats_landed(chunks, pairs):
                dve.wait_ge(x_stats, chunks)
                for buf in range(2):
                    dve.wait_ge(x1_stats[buf], pairs + 1)


            def finalise(step, first):
                base[0], links[0] = (step - 1) * STEPS + first, 0
                dve.memset(sm[:, :, :], 0.0)
                for n, st in enumerate((st_x, st_x1)):
                    for s in range(2):
                        ins = dve.bn_aggr(agg[:, n, s, :], st[:, s, :].rearrange("p (g k) -> p g k", k=6))
                link(ins)
                mean, spread, mean_h = agg[:, :, 0, 0], agg[:, :, 0, 1], agg[:, :, 1, 0]
                link(dve.tensor_tensor(sm[:, 0, :], mean_h, mean_h, ALU.mult))
                link(dve.tensor_tensor(sm[:, 1, :], spread, agg[:, :, 1, 1], ALU.add))
                link(dve.tensor_tensor(sm[:, 0, :], sm[:, 0, :], sm[:, 1, :], ALU.add))
                link(dve.tensor_tensor(sm[:, 1, :], mean, mean, ALU.mult))
                link(dve.tensor_copy(vec[:, 0, :], mean))
                dve.tensor_tensor(vec[:, 1, :], sm[:, 0, :], sm[:, 1, :], ALU.add).then_inc(vec_ready, 1)
                dve.wait_ge(group_sum, step)
                link(dve.tensor_copy(gst[:, :, :], ps_st[:, 0:4].rearrange("p (m n) -> p m n", m=2)))
                link(dve.tensor_tensor(sm[:, 0, :], gst[:, 0, :], gst[:, 0, :], ALU.mult))
                link(dve.tensor_tensor(sm[:, 1, :], gst[:, 1, :], tab("eps"), ALU.add))
                dve.tensor_tensor(var[:, :], sm[:, 1, :], sm[:, 0, :], ALU.subtract).then_inc(var_ready, 1)
                dve.wait_ge(pow_done, step)
                dve.tensor_tensor(rm[:, :], rstd[:, :], gst[:, 0, :], ALU.mult).then_inc(rm_ready, 1)
                for s in range(2):
                    ins = dve.scalar_tensor_tensor(wlh[:, s, :], mt[:, s, :], rstd[:, 0:1], tab("half"),
                                                   ALU.mult, ALU.add)
                ins.then_inc(wlh_ready, 1)
                dve.wait_ge(mean_mix, step)
                dve.tensor_tensor(bias[:, 0:1], bconst[:, 0:1], ps_st[:, 4:5], ALU.subtract).then_inc(bias_ready, 1)
                dve.wait_ge(rm_ready, step)
                link(dve.tensor_scalar(sm[:, 0, 0:1], rm[:, 1:2], float((2 * (H - 1)) * (2 * (W - 1))), None, ALU.mult))
                assert links[0] == STEPS

            def spectrum(b):
                dve.wait_ge(spec_stored, 32 * b + 32)
                for q in range(4):
                    dve.wait_ge(h_done, 8 * b + 2 * q + 2)
                    out = spec[:, :, :, 8 * q:8 * q + 8].rearrange("o h k l -> o l (h k)")
                    dve.tensor_scalar(out, ps_mix[q][0:C, :].rearrange("o (l k) -> o l k", l=8),
                                      rstd[0:C, 1:2], None, ALU.mult).then_inc(spec_read, 1)
                dve.wait_ge(spec_read, 4 * b + 8)
                dve.tensor_scalar(spec[:, 0, 0, 0:1], spec[:, 0, 0, 0:1], sm[0:C, 0, 0:1], None,
                                  ALU.subtract).then_inc(spec_ready, 1)

            with dve.Fori(0, PAIRS) as k:
                for buf in range(2):
                    dve.wait_ge(loaded[buf], 16 * k + 16)
                    low(2 * k + buf, buf)
                    stats_x(2 * k + buf, 2 * k + buf + 1)
            stats_landed(CHUNKS, 0)
            finalise(1, PROLOGUE)
            with dve.Fori(0, B - 1) as b:
                with dve.Fori(0, PAIRS) as k:
                    for buf in range(2):
                        dve.wait_ge(mixed, b * GROUPS + 4 * k + 2 * buf + 2)
                        dve.wait_ge(loaded[buf], (b * PAIRS + PAIRS + k) * 16 + 16)
                        low(2 * k + buf, buf)
                        stats_x(2 * k + buf, b * CHUNKS + CHUNKS + 2 * k + buf + 1)
                        stats_x1(k, buf, b * GROUPS + 4 * k + 2 * buf + 2)
                stats_landed(b * CHUNKS + 2 * CHUNKS, b * PAIRS + PAIRS)
                finalise(b + 2, PROLOGUE)
                spectrum(b)
            with dve.Fori(0, PAIRS) as k:
                for buf in range(2):
                    stats_x1(k, buf, (B - 1) * GROUPS + 4 * k + 2 * buf + 2)
            stats_landed(B * CHUNKS, B * PAIRS)
            finalise(B + 1, PROLOGUE)
            spectrum(B - 1)

        @block.tensor
        def _(pe):
            def mix(g, c, par, wait):
                wait()
                for s in range(2):
                    ins = pe.matmul(ps_mix[2 * par + s][:, :], wlh[:, s, :], lh[:, lh_cols(c, g, s)],
                                    start=True, stop=True)
                ins.then_inc(mixed, 1)

            def turn(buf, g, count, wait):
                pe.wait_ge(x1_ready, count)
                for pair in range(2):
                    wait(pair)
                    for r in range(2):
                        for s in range(2):
                            ins = pe.transpose(ps_t[pair][:, (2 * r + s) * P:(2 * r + s + 1) * P],
                                               x1[buf][:, GROUP * g + 2 * pair + r, s, :], tab("ident"))
                    ins.then_inc(turned, 1)

            def along_w(m, count):
                pe.wait_ge(x1t_ready, count)
                for pair in range(2):
                    for r in range(2):
                        col = (m * GROUP + 2 * pair + r) * MODES
                        for s in range(2):
                            ins = pe.matmul(ps_aw[:, col:col + MODES], x1t[pair][:, 2 * r + s, :],
                                            tab("dw")[:, s * MODES:(s + 1) * MODES],
                                            start=s == 0, stop=s == 1)
                ins.then_inc(w_done, 1)

            def moments(step):
                pe.wait_ge(vec_ready, step)
                pe.matmul(ps_st[:, 0:4], tab("gavg"), vec[:, :, :].rearrange("p m n -> p (m n)"),
                          start=True, stop=True).then_inc(group_sum, 1)
                pe.wait_ge(rm_ready, step)
                pe.matmul(ps_st[:, 4:5], mt[:, 0, :], rm[:, 0:1], start=True, stop=True).then_inc(mean_mix, 1)

            pe.wait_ge(mats_ready, 1)
            moments(1)
            with pe.Fori(0, B) as b:
                g0 = b * GROUPS

                def start_mix():
                    pe.wait_ge(wlh_ready, b + 1)
                    pe.wait_ge(spec_read, 4 * b + 4)

                mix(0, 0, 0, start_mix)
                mix(1, 0, 1, lambda: None)
                turn(0, 0, g0 + 1, lambda pair: pe.wait_ge(awt_ready, 8 * b + 8))
                with pe.Fori(0, PAIRS - 1) as k:
                    for m in range(4):
                        n = g0 + 4 * k + m
                        nx = m + 2
                        mix(nx % 2, 2 * k + nx // 2, nx % 2, lambda: pe.wait_ge(x1_ready, n + 1))
                        if m == 0:
                            pe.wait_ge(aw_ready, 8 * b + k + 8)
                        along_w(m, 2 * n + 2)
                        turn((m + 1) // 2 % 2, (m + 1) % 2, n + 2,
                             lambda pair: pe.wait_ge(x1t_ready, 2 * n + pair + 1))
                for m in range(4):
                    n = g0 + 4 * (PAIRS - 1) + m
                    nx = m + 2
                    if nx < 4:
                        mix(nx % 2, 2 * (PAIRS - 1) + nx // 2, nx % 2, lambda: pe.wait_ge(x1_ready, n + 1))
                    if m == 0:
                        pe.wait_ge(aw_ready, 8 * b + PAIRS - 1 + 8)
                    along_w(m, 2 * n + 2)
                    if m < 3:
                        turn((m + 1) // 2 % 2, (m + 1) % 2, n + 2,
                             lambda pair: pe.wait_ge(x1t_ready, 2 * n + pair + 1))
                pe.wait_ge(aw_ready, 8 * b + 16)

                def along_h(q):
                    pe.wait_ge(awt_ready, 8 * b + 8 + q + 1)
                    for j in range(4):
                        l8 = 4 * (q % 2) + j
                        for i in range(2):
                            ins = pe.matmul(ps_mix[q // 2][0:C, l8 * K2:(l8 + 1) * K2],
                                            awt[q % 2][:, j, C * i:C * i + C],
                                            tab("dh")[:, K2 * i:K2 * i + K2], start=i == 0, stop=i == 1)
                    ins.then_inc(h_done, 1)

                for q in range(MODES // 4):
                    if q >= 2:
                        pe.wait_ge(awt_ready, 8 * b + 8 + q - 1)
                    for j in range(4):
                        l = 4 * q + j
                        ins = pe.transpose(ps_t[q % 2][:, j * P:(j + 1) * P],
                                           aw[:, l:l + (HP - 1) * MODES + 1:MODES], tab("ident"))
                    ins.then_inc(aw_turned, 1)
                    if q >= 1:
                        along_h(q - 1)
                along_h(MODES // 4 - 1)
                moments(b + 2)

        @block.scalar
        def _(act):
            act.sem_inc(aw_ready, 8)
            act.sem_inc(awt_ready, 8)
            act.sem_inc(spec_read, 4)

            def take(par, buf, g, count, wait):
                act.wait_ge(mixed, count)
                wait()
                for s in range(2):
                    ins = act.activation(x1[buf][:, GROUP * g:GROUP * g + GROUP, s, :],
                                         ps_mix[2 * par + s][:, :].rearrange("p (r w) -> p r w", w=WP),
                                         ACT.Identity, bias=bias[:, s:s + 1])
                ins.then_inc(x1_ready, 1)

            def take_turned(count, done):
                for pair in range(2):
                    act.wait_ge(turned, 2 * count - 1 + pair)
                    if pair == 0:
                        act.wait_ge(w_done, done)
                    act.activation(x1t[pair][:, :, :].rearrange("p a q -> p (a q)"), ps_t[pair][:, :],
                                   ACT.Copy).then_inc(x1t_ready, 1)

            def buffer_free(use, buf):
                act.wait_ge(stored[buf], 16 * use + 16)
                act.wait_ge(x1_stats[buf], use + 1)

            act.sem_inc(w_done, 1)
            act.sem_inc(spec_stored, 32)

            with act.Fori(0, B) as b:
                g0 = b * GROUPS
                act.wait_ge(bias_ready, b + 1)
                take(0, 0, 0, g0 + 1, lambda: buffer_free(b * PAIRS, 0))
                take(1, 0, 1, g0 + 2, lambda: None)
                take_turned(g0 + 1, g0 + 1)
                with act.Fori(0, PAIRS - 1) as k:
                    for m in range(4):
                        n = g0 + 4 * k + m
                        nx = m + 2
                        buf = nx // 2 % 2
                        use = b * PAIRS + k + nx // 4

                        def free():
                            if nx % 2 == 0:
                                buffer_free(use, buf)
                        take(nx % 2, buf, nx % 2, n + 3, free)
                        take_turned(n + 2, n + 2)
                        if m == 3:
                            act.wait_ge(w_done, n + 2)
                            act.activation(aw[:, ds(k * 512, 512)], ps_aw[:, :], ACT.Copy).then_inc(aw_ready, 1)
                for m in range(4):
                    n = g0 + 4 * (PAIRS - 1) + m
                    nx = m + 2
                    if nx < 4:
                        def free():
                            if nx % 2 == 0:
                                buffer_free(b * PAIRS + PAIRS - 1, 1)
                        take(nx % 2, nx // 2 % 2, nx % 2, n + 3, free)
                    if m < 3:
                        take_turned(n + 2, n + 2)
                act.wait_ge(w_done, g0 + GROUPS + 1)
                act.activation(aw[:, (PAIRS - 1) * 512:PAIRS * 512], ps_aw[:, :], ACT.Copy).then_inc(aw_ready, 1)
                for q in range(MODES // 4):
                    act.wait_ge(aw_turned, 8 * b + q + 1)
                    if q >= 2:
                        act.wait_ge(h_done, 8 * b + q - 1)
                    act.activation(awt[q % 2][:, :, :].rearrange("p a q -> p (a q)"), ps_t[q % 2][:, :],
                                   ACT.Copy).then_inc(awt_ready, 1)
                act.wait_ge(spec_ready, b + 1)
                for half in range(2):
                    act.dma_start(spec_scr[:, half, :, ds(b, 1), :].rearrange("c o b m -> o c (b m)"),
                                  spec[:, half, :, :].rearrange("o (c k) l -> o c (k l)", k=4)).then_inc(spec_stored, 16)
            act.wait_ge(spec_stored, 32 * B + 32)


def stage_two(nc, weights, spec_scr, f_scr):
    with ExitStack() as ctx:
        def sb(name, shape):
            return ctx.enter_context(nc.sbuf_tensor(name, shape, F32))

        def sem(name):
            return ctx.enter_context(nc.semaphore(name))

        wq = [sb(f"wq{i}", [P, 4, MODES, C]) for i in range(2)]
        sq = [sb(f"sq{i}", [P, 32, 4 * MODES]) for i in range(2)]
        fo = [sb(f"fo{i}", [P, 4, 512]) for i in range(2)]
        ps = [ctx.enter_context(nc.psum_tensor(f"ps_f{i}", [P, 512], F32)) for i in range(8)]
        cleared = sem("sq_cleared")
        w_in = [sem(f"wq_in{i}") for i in range(2)]
        s_in = [sem(f"sq_in{i}") for i in range(2)]
        done = sem("modes_done")
        act_read = sem("f_act_read")
        dve_read = sem("f_dve_read")
        f_stored = [sem(f"f_stored{i}") for i in range(2)]
        block = ctx.enter_context(nc.Block())
        TURNS = QUADS // 2

        @block.sync
        def _(sp):
            for par in range(2):
                sp.sem_inc(f_stored[par], 128)

            def load(row, par):
                sp.dma_start(wq[par][:, :, :, :].rearrange("p k l o -> p (k l o)"),
                             weights[row, :, :].rearrange("a p m -> p (a m)")).then_inc(w_in[par], 16)
                for half in range(2):
                    sp.dma_start(sq[par][C * half:C * half + C, B * half:B * half + B, :],
                                 spec_scr[row, half, :, :, :].rearrange("a o b m -> (a o) b m"))\
                      .then_inc(s_in[par], 16)

            def store(kq, par):
                sp.wait_ge(act_read, 4 * kq + 2 * par + 2 + 4)
                sp.wait_ge(dve_read, 4 * kq + 2 * par + 2 + 4)
                for g in range(4):
                    for half in range(2):
                        first = 32 * g + B * half
                        k = ds(half * MODES + 4 * (2 * kq + par) + g, 1)
                        sp.dma_start(f_scr[:, :, k, :].rearrange("b l k o -> b l (k o)"),
                                     fo[par][first:first + B, :, :].rearrange("b q (l o) -> b (q l) o", o=C))\
                          .then_inc(f_stored[par], 16)

            sp.wait_ge(cleared, 2)
            for par in range(2):
                load(ds(par, 1), par)
            with sp.Fori(0, TURNS - 1) as kq:
                for par in range(2):
                    sp.wait_ge(done, 8 * kq + 4 * par + 4)
                    load(ds(2 * kq + 2 + par, 1), par)
                    store(kq, par)
            for par in range(2):
                store(TURNS - 1, par)
            for par in range(2):
                sp.wait_ge(f_stored[par], 128 * TURNS + 128)

        @block.tensor
        def _(pe):
            with pe.Fori(0, TURNS) as kq:
                for par in range(2):
                    pe.wait_ge(w_in[par], 16 * kq + 16)
                    pe.wait_ge(s_in[par], 32 * kq + 32)
                    for octet in range(4):
                        pe.wait_ge(act_read if octet < 2 else dve_read, 4 * kq + 2 * par + octet % 2 + 1)
                        for l8 in range(8):
                            for g in range(4):
                                l = 8 * octet + l8
                                ins = pe.matmul(ps[4 * par + octet][32 * g:32 * g + 32, l8 * C:(l8 + 1) * C],
                                                sq[par][:, :, g * MODES + l], wq[par][:, g, l, :],
                                                start=True, stop=True)
                        ins.then_inc(done, 1)

        def copies(eng, octets, read, copy):
            eng.sem_inc(read, 4)
            with eng.Fori(0, TURNS) as kq:
                for par in range(2):
                    eng.wait_ge(f_stored[par], 128 * kq + 128)
                    for octet in octets:
                        eng.wait_ge(done, 8 * kq + 4 * par + octet + 1)
                        copy(fo[par][:, octet, :], ps[4 * par + octet][:, :]).then_inc(read, 1)

        @block.scalar
        def _(act):
            copies(act, (0, 1), act_read, lambda out, in_: act.activation(out, in_, ACT.Copy))

        @block.vector
        def _(dve):
            for par in range(2):
                dve.memset(sq[par][:, :, :], 0.0).then_inc(cleared, 1)
            copies(dve, (2, 3), dve_read, lambda out, in_: dve.tensor_copy(out, in_))


def stage_three(nc, tab, x1_scr, f_scr, out):
    with ExitStack() as ctx:
        def sb(name, shape):
            return ctx.enter_context(nc.sbuf_tensor(name, shape, F32))

        def sem(name):
            return ctx.enter_context(nc.semaphore(name))

        f = sb("f", [MODES, K2, C])
        fq = [sb(f"fq{i}", [MODES, 8, K2]) for i in range(2)]
        gw = [sb(f"gw{i}", [P, 4, W]) for i in range(2)]
        xt = [sb(f"xt{i}", [P, 8, W]) for i in range(4)]
        ot = [sb(f"ot{i}", [P, 8, 2, WP]) for i in range(4)]
        ps_g = [ctx.enter_context(nc.psum_tensor(f"ps_g{i}", [P, 512], F32)) for i in range(4)]
        ps_o = [ctx.enter_context(nc.psum_tensor(f"ps_o{i}", [P, 1024], F32)) for i in range(2)]
        f_in = sem("f_in")
        fq_ready = sem("fq_ready")
        g_done = sem("g_done")
        gw_ready = sem("gw_ready")
        h_out = sem("h_out")
        x1_in = [sem(f"x1_in{i}") for i in range(4)]
        added = sem("added")
        even_done = sem("even_done")
        odd_done = sem("odd_done")
        out_stored = [sem(f"out_stored{i}") for i in range(4)]
        block = ctx.enter_context(nc.Block())
        STEPS = B * OCT
        TURNS = STEPS // 2

        @block.sync
        def _(sp):
            for buf in range(4):
                sp.sem_inc(out_stored[buf], 16)

            def load(rows, octet, buf):
                cols = ds((buf % 2 * C + 8 * octet) * W, 8 * W)
                sp.dma_start(xt[buf][:, :, :].rearrange("p o w -> p (o w)"), x1_scr[rows, cols])\
                  .then_inc(x1_in[buf], 16)

            def store(turn, buf):
                sp.wait_ge(even_done, 4 * turn + buf + 1)
                sp.wait_ge(odd_done, 4 * turn + buf + 1)
                sp.dma_start(out[ds(4 * turn + buf, 1), :, :].rearrange("a p m -> p (a m)"),
                             ot[buf][:, :, :, :].rearrange("p o j w -> p (o j w)")).then_inc(out_stored[buf], 16)

            PER = OCT // 2
            for buf in range(4):
                load(ds(0, HP), buf // 2, buf)
            with sp.Fori(0, B - 1) as b:
                with sp.Fori(0, PER - 1) as t:
                    for buf in range(4):
                        store(b * PER + t, buf)
                        load(ds(b * HP, HP), 2 * t + 2 + buf // 2, buf)
                for buf in range(4):
                    store(b * PER + PER - 1, buf)
                    load(ds(b * HP + HP, HP), buf // 2, buf)
            with sp.Fori(0, PER - 1) as t:
                for buf in range(4):
                    store((B - 1) * PER + t, buf)
                    load(ds((B - 1) * HP, HP), 2 * t + 2 + buf // 2, buf)
            for buf in range(4):
                store(B * PER - 1, buf)
            for buf in range(4):
                sp.wait_ge(out_stored[buf], 16 * TURNS + 16)

        @block.tensor
        def _(pe):
            def along_w(step, par):
                pe.wait_ge(fq_ready, step + 1)
                for half in range(2):
                    pe.wait_ge(gw_ready, 2 * step + half + 1)
                    for j in range(2):
                        ins = pe.matmul(ps_g[2 * par + half][:, j * W:(j + 1) * W],
                                        fq[par][:, 4 * half + 2 * j:4 * half + 2 * j + 2, :],
                                        tab("cw")[0:MODES, :], start=True, stop=True)
                    ins.then_inc(g_done, 1)

            def along_h(step, par):
                pe.wait_ge(gw_ready, 2 * step + 2 + 4)
                for i in range(2):
                    for r in range(2):
                        pe.wait_ge(added, 4 * step + 2 * i + r + 1)
                        rows = slice(K2 * r, K2 * r + K2)
                        for half in range(2):
                            ins = pe.matmul(ps_o[r][:, half * 512:half * 512 + 512],
                                            tab("ch")[rows, i * HP:(i + 1) * HP],
                                            gw[par][rows, 2 * half:2 * half + 2, :], start=True, stop=True)
                        ins.then_inc(h_out, 1)

            along_w(0, 0)
            with pe.Fori(0, TURNS - 1) as t:
                along_w(2 * t + 1, 1)
                along_h(2 * t, 0)
                along_w(2 * t + 2, 0)
                along_h(2 * t + 1, 1)
            along_w(STEPS - 1, 1)
            along_h(STEPS - 2, 0)
            along_h(STEPS - 1, 1)

        @block.scalar
        def _(act):
            act.sem_inc(gw_ready, 4)
            act.sem_inc(h_out, 8)

            def load_f(row):
                act.dma_start(f[:, :, :], f_scr[row, :, :, :].rearrange("a l k o -> (a l) k o")).then_inc(f_in, 16)

            def pick(step, octet, par):
                act.activation(fq[par][:, :, :], f[:, :, ds(octet * 8, 8)].rearrange("l k o -> l o k"),
                               ACT.Copy).then_inc(fq_ready, 1)

            def take(step, par):
                act.wait_ge(h_out, 4 * step + 4)
                for half in range(2):
                    act.wait_ge(g_done, 2 * step + half + 1)
                    act.activation(gw[par][:, 2 * half:2 * half + 2, :].rearrange("p j w -> p (j w)"),
                                   ps_g[2 * par + half][:, :], ACT.Copy).then_inc(gw_ready, 1)

            def element(b, following):
                act.wait_ge(f_in, 16 * b + 16)
                with act.Fori(0, OCT // 2 - 1) as t:
                    for par in range(2):
                        pick(b * OCT + 2 * t + par, 2 * t + par, par)
                        take(b * OCT + 2 * t + par, par)
                pick(b * OCT + OCT - 2, OCT - 2, 0)
                take(b * OCT + OCT - 2, 0)
                pick(b * OCT + OCT - 1, OCT - 1, 1)
                if following is not None:
                    act.wait_ge(fq_ready, b * OCT + OCT)
                    load_f(following)
                take(b * OCT + OCT - 1, 1)

            load_f(ds(0, 1))
            with act.Fori(0, B - 1) as b:
                element(b, ds(b + 1, 1))
            element(B - 1, None)

        @block.vector
        def _(dve):
            dve.sem_inc(added, 2)
            with dve.Fori(0, TURNS) as t:
                for buf in range(4):
                    unit = 4 * t + buf
                    dve.wait_ge(x1_in[buf], 16 * t + 16)
                    v = xt[buf][:, :, :].rearrange("p (j r) w -> p r j w", r=2)
                    for r in range(2):
                        dve.wait_ge(h_out, 2 * unit + r + 1 + 8)
                        dve.tensor_tensor(v[:, r, :, :], v[:, r, :, :],
                                          ps_o[r][:, :].rearrange("p (j w) -> p j w", w=W), ALU.add)\
                           .then_inc(added, 1)
                    dve.wait_ge(added, 2 * unit + 2 + 2)
                    dve.wait_ge(out_stored[buf], 16 * t + 16)
                    dve.tensor_tensor(ot[buf][:, :, 0, :], xt[buf][:, :, 0:WP], xt[buf][:, :, WP:W],
                                      ALU.add).then_inc(even_done, 1)

        @block.gpsimd
        def _(pool):
            with pool.Fori(0, TURNS) as t:
                for buf in range(4):
                    pool.wait_ge(added, 2 * (4 * t + buf) + 2 + 2)
                    pool.wait_ge(out_stored[buf], 16 * t + 16)
                    pool.tensor_tensor(ot[buf][:, :, 1, :], xt[buf][:, :, 0:WP], xt[buf][:, :, WP:W],
                                       ALU.subtract).then_inc(odd_done, 1)


def build(nc, x, mix_t, biases, weights, constants, out):
    x1_scr = nc.dram_tensor("x1_scr", (B * HP, HPITCH), F32, kind="Internal").ap()
    spec_scr = nc.dram_tensor("spec_scr", (QUADS, 2, C, B, 4 * MODES), F32, kind="Internal").ap()
    f_scr = nc.dram_tensor("f_scr", (B, MODES, K2, C), F32, kind="Internal").ap()
    with nc.sbuf_tensor("table", [P, TABLE_COLS], F32) as table:
        def tab(name):
            lo, hi = TABLE[name]
            return table[:, lo:hi]

        with nc.semaphore("table_in") as table_in, nc.Block() as block:
            @block.sync
            def _(sp):
                sp.dma_start(table[:, :], constants).then_inc(table_in, 16)
                sp.wait_ge(table_in, 16)
        stage_one(nc, tab, x, mix_t, biases, x1_scr, spec_scr)
        stage_two(nc, weights, spec_scr, f_scr)
        stage_three(nc, tab, x1_scr, f_scr, out)


def kernel(x, L0_conv_w_LL, L0_conv_b_LL, L0_conv_w_LH, L0_conv_b_LH, L0_conv_w_HL, L0_conv_b_HL,
           L0_conv_w_HH, L0_conv_b_HH, L1_conv_weights1, L1_conv_weights2):
    import concourse.bacc as bacc
    from concourse.bass_utils import run_bass_kernel_spmd

    a = np.asarray
    xs = a(x).reshape(B, C, CHUNKS, CHUNK, 2, WP, 2).transpose(0, 2, 4, 1, 3, 6, 5)
    mix = np.stack([a(w).T for w in (L0_conv_w_LL, L0_conv_w_LH, L0_conv_w_HL, L0_conv_w_HH)], axis=1)
    biases = np.stack([a(v) for v in (L0_conv_b_LL, L0_conv_b_LH, L0_conv_b_HL, L0_conv_b_HH)], axis=1)
    ws = np.stack([a(L1_conv_weights1), a(L1_conv_weights2)])
    ws = ws.reshape(2, C, C, QUADS, 4, MODES).transpose(3, 0, 1, 4, 5, 2)
    arrays = {
        "x": np.ascontiguousarray(xs).reshape(B * CHUNKS, P, CHUNK * W),
        "mix_t": np.ascontiguousarray(mix),
        "biases": np.ascontiguousarray(biases),
        "weights": np.ascontiguousarray(ws).reshape(QUADS, P, 4 * MODES * C),
        "constants": table_of_constants(),
    }
    nc = bacc.Bacc("TRN2", target_bir_lowering=False, num_devices=1)
    args = [nc.dram_tensor(name, v.shape, F32, kind="ExternalInput").ap() for name, v in arrays.items()]
    out = nc.dram_tensor("out", (B * OCT * 2, P, 8 * W), F32, kind="ExternalOutput").ap()
    build(nc, *args, out)
    got = run_bass_kernel_spmd(nc, [arrays], core_ids=[0]).results[0]["out"]
    got = got.reshape(B, OCT, 2, HP, 8, 2, WP).transpose(0, 1, 4, 3, 2, 6, 5)
    return np.ascontiguousarray(got).reshape(B, C, H, W)
```

```python
from contextlib import ExitStack

import concourse.bass as bass
from concourse import mybir
import numpy as np

F32 = mybir.dt.float32
F32R = mybir.dt.float32r
ALU = mybir.AluOpType
ACT = mybir.ActivationFunctionType
ds = bass.ds

P = 128
B, C, H, W = 8, 64, 256, 256
MODES = 32
HP, WP = H // 2, W // 2
K2 = 2 * MODES
CHUNK = 8
CHUNKS = HP // CHUNK
PAIRS = CHUNKS // 2
GROUP = 4
GROUPS = HP // GROUP
GCOLS = GROUP * WP
QUADS = MODES // 4
EPS = 1e-5
HPITCH = P * W + 1024
OCT = C // 8

TABLE = {}
_at = 0
for _name, _width in (("ident", P), ("gavg", P), ("half", P), ("dw", 2 * MODES), ("dh", 2 * K2),
                      ("ch", 4 * HP), ("cw", 4 * WP), ("sign", 2), ("eps", 2), ("power", 2)):
    TABLE[_name] = (_at, _at + _width)
    _at += _width
TABLE_COLS = _at


def split(a):
    a = a.astype(np.float32)
    top = ((a.view(np.uint32) + np.uint32(0x800)) & np.uint32(0xFFFFF000)).view(np.float32)
    return top, a - top


def table_of_constants():
    t = np.zeros((P, TABLE_COLS), np.float64)

    def put(name, a, rows=slice(0, P)):
        lo, hi = TABLE[name]
        t[rows, lo:hi] = a.reshape(a.shape[0], -1)

    part = np.arange(P)
    put("ident", np.eye(P))
    group = (part % C) // 2
    put("gavg", (group[:, None] == group[None, :]) / 4.0)
    put("half", 0.5 * np.eye(P))
    rows = np.concatenate([np.arange(MODES), H - MODES + np.arange(MODES)])
    space = np.arange(H)
    cosines = np.cos(np.pi * ((rows[:, None] * space[None, :]) % (2 * (H - 1))) / (H - 1))
    ends_space = np.where((space == 0) | (space == H - 1), 1.0, 2.0)
    ends_rows = np.where((rows == 0) | (rows == H - 1), 1.0, 2.0)
    forward = cosines * ends_space[None, :]
    inverse = cosines * ends_rows[:, None]
    even, odd = forward[:MODES, 0::2], forward[:MODES, 1::2]
    put("dw", np.stack([even + odd, even - odd]).transpose(2, 0, 1))
    put("dh", np.stack([forward[:, 0::2], forward[:, 1::2]]).transpose(2, 0, 1))
    ch = np.stack([inverse[:, 0::2], inverse[:, 1::2]], axis=1)
    put("ch", np.tile(np.stack(split(ch), axis=1), (2, 1, 1, 1)))
    even, odd = inverse[:MODES, 0::2], inverse[:MODES, 1::2]
    cw = np.stack([(even + odd) / 2, (even - odd) / 2], axis=1)
    put("cw", np.tile(np.stack(split(cw), axis=1), (2, 1, 1, 1)), slice(0, 2 * MODES))
    upper = np.where(part < C, 1.0, -1.0)
    put("sign", np.stack([upper, -upper], axis=1))
    put("eps", np.tile([[4 * EPS, EPS]], (P, 1)))
    put("power", np.full((P, 2), -0.5))
    return t.astype(np.float32)


def stage_one(nc, tab, x, mix_t, biases, x1_scr, spec_scr):
    with ExitStack() as ctx:
        def sb(name, shape):
            return ctx.enter_context(nc.sbuf_tensor(name, shape, F32))

        def sem(name):
            return ctx.enter_context(nc.semaphore(name))

        raw = [sb(f"raw{i}", [P, CHUNK, 2, WP]) for i in range(2)]
        lh = sb("lh", [P, CHUNKS * 2 * 2 * GCOLS])
        x1 = [sb(f"x1_{i}", [P, CHUNK, 2, WP]) for i in range(2)]
        x1t = [sb(f"x1t{i}", [P, 4, P]) for i in range(2)]
        aw = sb("aw", [P, HP * MODES])
        awt = [sb(f"awt{i}", [P, 4, P]) for i in range(2)]
        spec = sb("spec", [C, 2, MODES, MODES])
        wraw = sb("wraw", [P, 4, C])
        mt = sb("mt", [P, 2, P])
        wlh = sb("wlh", [P, 2, P])
        braw = sb("braw", [P, 4])
        bconst = sb("bconst", [P, 2])
        bias = sb("bias", [P, 2])
        st_x = sb("st_x", [P, 2, GROUPS * 6])
        st_x1 = sb("st_x1", [P, 2, GROUPS * 6])
        agg = sb("agg", [P, 2, 2, 2])
        vec = sb("vec", [P, 2, 2])
        gst = sb("gst", [P, 2, 2])
        sm = sb("sm", [P, 2, 2])
        var = sb("var", [P, 2])
        rstd = sb("rstd", [P, 2])
        rm = sb("rm", [P, 2])

        ps_mix = [ctx.enter_context(nc.psum_tensor(f"ps_mix{i}", [P, 512], F32)) for i in range(4)]
        ps_t = [ctx.enter_context(nc.psum_tensor(f"ps_t{i}", [P, 512], F32)) for i in range(2)]
        ps_aw = ctx.enter_context(nc.psum_tensor("ps_aw", [P, 512], F32))
        ps_st = ctx.enter_context(nc.psum_tensor("ps_st", [P, 512], F32))

        params_in = sem("params_in")
        mats_ready = sem("mats_ready")
        loaded = [sem(f"loaded{i}") for i in range(2)]
        low_done = sem("low_done")
        high_done = sem("high_done")
        vec_ready = sem("vec_ready")
        group_sum = sem("group_sum")
        var_ready = sem("var_ready")
        pow_done = sem("pow_done")
        rm_ready = sem("rm_ready")
        mean_mix = sem("mean_mix")
        wlh_ready = sem("wlh_ready")
        bias_ready = sem("bias_ready")
        mixed = sem("mixed")
        x1_ready = sem("x1_ready")
        x_stats = sem("x_stats")
        x1_stats = [sem(f"x1_stats{i}") for i in range(2)]
        stored = [sem(f"stored{i}") for i in range(2)]
        turned = sem("turned")
        x1t_ready = sem("x1t_ready")
        w_done = sem("w_done")
        aw_ready = sem("aw_ready")
        aw_turned = sem("aw_turned")
        awt_ready = sem("awt_ready")
        h_done = sem("h_done")
        spec_read = sem("spec_read")
        spec_ready = sem("spec_ready")
        spec_stored = sem("spec_stored")
        chain = sem("chain")

        def lh_cols(c, g, s, cols=GCOLS):
            return ds(c * (4 * GCOLS) + (g * 2 + s) * GCOLS, cols)

        block = ctx.enter_context(nc.Block())

        @block.sync
        def _(sp):
            for buf in range(2):
                sp.sem_inc(stored[buf], 16)
            for half in range(2):
                sp.dma_start(wraw[C * half:C * half + C], mix_t).then_inc(params_in, 16)
                sp.dma_start(braw[C * half:C * half + C], biases).then_inc(params_in, 16)

            def load(row, buf):
                sp.dma_start(raw[buf][:, :, :, :].rearrange("p r j w -> p (r j w)"), x[row, :, :].rearrange("a p m -> p (a m)")).then_inc(loaded[buf], 16)

            for buf in range(2):
                load(ds(buf, 1), buf)
            with sp.Fori(1, PAIRS) as k:
                for buf in range(2):
                    sp.wait_ge(low_done, 2 * k + buf - 1)
                    sp.wait_ge(high_done, 2 * k + buf - 1)
                    load(ds(2 * k + buf, 1), buf)

            def store(row, count, buf):
                sp.wait_ge(x1_ready, count)
                sp.dma_start(x1_scr[row, 0:P * W].rearrange("r (p w) -> p r w", w=W),
                             x1[buf][:, :, :, :].rearrange("p r j w -> p r (j w)")).then_inc(stored[buf], 16)

            with sp.Fori(0, PAIRS * (B - 1)) as k:
                for buf in range(2):
                    sp.wait_ge(low_done, 2 * k + CHUNKS + buf - 1)
                    sp.wait_ge(high_done, 2 * k + CHUNKS + buf - 1)
                    load(ds(2 * k + CHUNKS + buf, 1), buf)
                for buf in range(2):
                    store(ds((2 * k + buf) * CHUNK, CHUNK), 4 * k + 2 * buf + 2, buf)
            with sp.Fori(PAIRS * (B - 1), PAIRS * B) as k:
                for buf in range(2):
                    store(ds((2 * k + buf) * CHUNK, CHUNK), 4 * k + 2 * buf + 2, buf)
            for buf in range(2):
                sp.wait_ge(stored[buf], 16 * (PAIRS * B) + 16)

        @block.gpsimd
        def _(pool):
            def high(c, buf):
                v = raw[buf][:, :, :, :]
                for g in range(2):
                    out = lh[:, lh_cols(c, g, 1)].rearrange("p (r w) -> p r w", w=WP)
                    rows = slice(GROUP * g, GROUP * g + GROUP)
                    ins = pool.tensor_tensor(out, v[:, rows, 0, :], v[:, rows, 1, :], ALU.subtract)
                ins.then_inc(high_done, 1)

            def power(step):
                pool.wait_ge(var_ready, step)
                pool.tensor_tensor(rstd[:, :], var[:, :], tab("power"), ALU.pow).then_inc(pow_done, 1)

            pool.wait_ge(mats_ready, 1)
            with pool.Fori(0, PAIRS) as k:
                for buf in range(2):
                    pool.wait_ge(loaded[buf], 16 * k + 16)
                    high(2 * k + buf, buf)
            power(1)
            with pool.Fori(0, B - 1) as b:
                with pool.Fori(0, PAIRS) as k:
                    for buf in range(2):
                        pool.wait_ge(mixed, b * GROUPS + 4 * k + 2 * buf + 2)
                        pool.wait_ge(loaded[buf], (b * PAIRS + PAIRS + k) * 16 + 16)
                        high(2 * k + buf, buf)
                power(b + 2)
            power(B + 1)

        @block.vector
        def _(dve):
            links = [0]

            def link(ins):
                links[0] += 1
                ins.then_inc(chain, 1)
                dve.wait_ge(chain, links[0] if base[0] is None else base[0] + links[0])

            base = [None]

            for buf in range(2):
                dve.sem_inc(x1_stats[buf], 1)
            for half in range(2):
                dve.memset(st_x1[:, half, :], 1.0).then_inc(chain, 1)
            links[0] = 2
            dve.wait_ge(chain, 2)
            dve.wait_ge(params_in, 16 * 4)
            for s in range(2):
                lo, hi = wraw[:, 2 * s, :], wraw[:, 2 * s + 1, :]
                for i in range(2):
                    link(dve.scalar_tensor_tensor(mt[:, s, C * i:C * i + C], hi, tab("sign")[:, i:i + 1], lo,
                                                  ALU.mult, ALU.add))
                link(dve.scalar_tensor_tensor(bconst[:, s:s + 1], braw[:, 2 * s + 1:2 * s + 2],
                                              tab("sign")[:, 0:1], braw[:, 2 * s:2 * s + 1], ALU.mult, ALU.add))
            link(dve.tensor_scalar(mt[:, :, :], mt[:, :, :], 0.5, None, ALU.mult))
            link(dve.tensor_scalar(bconst[:, :], bconst[:, :], 0.5, None, ALU.mult))
            link(dve.tensor_copy(bias[:, 1:2], bconst[:, 1:2]))
            dve.sem_inc(mats_ready, 1)
            PROLOGUE = links[0]

            def low(c, buf):
                v = raw[buf][:, :, :, :]
                for g in range(2):
                    out = lh[:, lh_cols(c, g, 0)].rearrange("p (r w) -> p r w", w=WP)
                    rows = slice(GROUP * g, GROUP * g + GROUP)
                    ins = dve.tensor_tensor(out, v[:, rows, 0, :], v[:, rows, 1, :], ALU.add)
                ins.then_inc(low_done, 1)

            def stats_x(c, n):
                dve.wait_ge(low_done, n)
                dve.wait_ge(high_done, n)
                for g in range(2):
                    for s in range(2):
                        ins = dve.bn_stats(st_x[:, s, ds(c * 12 + g * 6, 6)], lh[:, lh_cols(c, g, s)])
                ins.then_inc(x_stats, 1)

            def stats_x1(k, buf, count):
                dve.wait_ge(x1_ready, count)
                for g in range(2):
                    for s in range(2):
                        ins = dve.bn_stats(st_x1[:, s, ds(k * 24 + buf * 12 + g * 6, 6)],
                                           x1[buf][:, GROUP * g:GROUP * g + GROUP, s, :])
                ins.then_inc(x1_stats[buf], 1)

            STEPS = 10

            def stats_landed(chunks, pairs):
                dve.wait_ge(x_stats, chunks)
                for buf in range(2):
                    dve.wait_ge(x1_stats[buf], pairs + 1)


            def finalise(step, first):
                base[0], links[0] = (step - 1) * STEPS + first, 0
                dve.memset(sm[:, :, :], 0.0)
                for n, st in enumerate((st_x, st_x1)):
                    for s in range(2):
                        ins = dve.bn_aggr(agg[:, n, s, :], st[:, s, :].rearrange("p (g k) -> p g k", k=6))
                link(ins)
                mean, spread, mean_h = agg[:, :, 0, 0], agg[:, :, 0, 1], agg[:, :, 1, 0]
                link(dve.tensor_tensor(sm[:, 0, :], mean_h, mean_h, ALU.mult))
                link(dve.tensor_tensor(sm[:, 1, :], spread, agg[:, :, 1, 1], ALU.add))
                link(dve.tensor_tensor(sm[:, 0, :], sm[:, 0, :], sm[:, 1, :], ALU.add))
                link(dve.tensor_tensor(sm[:, 1, :], mean, mean, ALU.mult))
                link(dve.tensor_copy(vec[:, 0, :], mean))
                dve.tensor_tensor(vec[:, 1, :], sm[:, 0, :], sm[:, 1, :], ALU.add).then_inc(vec_ready, 1)
                dve.wait_ge(group_sum, step)
                link(dve.tensor_copy(gst[:, :, :], ps_st[:, 0:4].rearrange("p (m n) -> p m n", m=2)))
                link(dve.tensor_tensor(sm[:, 0, :], gst[:, 0, :], gst[:, 0, :], ALU.mult))
                link(dve.tensor_tensor(sm[:, 1, :], gst[:, 1, :], tab("eps"), ALU.add))
                dve.tensor_tensor(var[:, :], sm[:, 1, :], sm[:, 0, :], ALU.subtract).then_inc(var_ready, 1)
                dve.wait_ge(pow_done, step)
                dve.tensor_tensor(rm[:, :], rstd[:, :], gst[:, 0, :], ALU.mult).then_inc(rm_ready, 1)
                for s in range(2):
                    ins = dve.scalar_tensor_tensor(wlh[:, s, :], mt[:, s, :], rstd[:, 0:1], tab("half"),
                                                   ALU.mult, ALU.add)
                ins.then_inc(wlh_ready, 1)
                dve.wait_ge(mean_mix, step)
                dve.tensor_tensor(bias[:, 0:1], bconst[:, 0:1], ps_st[:, 4:5], ALU.subtract).then_inc(bias_ready, 1)
                dve.wait_ge(rm_ready, step)
                link(dve.tensor_scalar(sm[:, 0, 0:1], rm[:, 1:2], float((2 * (H - 1)) * (2 * (W - 1))), None, ALU.mult))
                assert links[0] == STEPS

            def spectrum(b):
                dve.wait_ge(spec_stored, 32 * b + 32)
                for q in range(4):
                    dve.wait_ge(h_done, 8 * b + 2 * q + 2)
                    out = spec[:, :, 8 * q:8 * q + 8, :].rearrange("o h l k -> o l h k")
                    dve.tensor_scalar(out, ps_mix[q][0:C, :].rearrange("o (l h k) -> o l h k", l=8, h=2),
                                      rstd[0:C, 1:2], None, ALU.mult).then_inc(spec_read, 1)
                dve.wait_ge(spec_read, 4 * b + 8)
                dve.tensor_scalar(spec[:, 0, 0, 0:1], spec[:, 0, 0, 0:1], sm[0:C, 0, 0:1], None,
                                  ALU.subtract).then_inc(spec_ready, 1)

            with dve.Fori(0, PAIRS) as k:
                for buf in range(2):
                    dve.wait_ge(loaded[buf], 16 * k + 16)
                    low(2 * k + buf, buf)
                    stats_x(2 * k + buf, 2 * k + buf + 1)
            stats_landed(CHUNKS, 0)
            finalise(1, PROLOGUE)
            with dve.Fori(0, B - 1) as b:
                with dve.Fori(0, PAIRS) as k:
                    for buf in range(2):
                        dve.wait_ge(mixed, b * GROUPS + 4 * k + 2 * buf + 2)
                        dve.wait_ge(loaded[buf], (b * PAIRS + PAIRS + k) * 16 + 16)
                        low(2 * k + buf, buf)
                        stats_x(2 * k + buf, b * CHUNKS + CHUNKS + 2 * k + buf + 1)
                        stats_x1(k, buf, b * GROUPS + 4 * k + 2 * buf + 2)
                stats_landed(b * CHUNKS + 2 * CHUNKS, b * PAIRS + PAIRS)
                finalise(b + 2, PROLOGUE)
                spectrum(b)
            with dve.Fori(0, PAIRS) as k:
                for buf in range(2):
                    stats_x1(k, buf, (B - 1) * GROUPS + 4 * k + 2 * buf + 2)
            stats_landed(B * CHUNKS, B * PAIRS)
            finalise(B + 1, PROLOGUE)
            spectrum(B - 1)

        @block.tensor
        def _(pe):
            def mix(g, c, par, wait):
                wait()
                for s in range(2):
                    ins = pe.matmul(ps_mix[2 * par + s][:, :], wlh[:, s, :], lh[:, lh_cols(c, g, s)],
                                    start=True, stop=True)
                ins.then_inc(mixed, 1)

            def turn(buf, g, count, wait):
                pe.wait_ge(x1_ready, count)
                for pair in range(2):
                    wait(pair)
                    for r in range(2):
                        for s in range(2):
                            ins = pe.transpose(ps_t[pair][:, (2 * r + s) * P:(2 * r + s + 1) * P],
                                               x1[buf][:, GROUP * g + 2 * pair + r, s, :], tab("ident"))
                    ins.then_inc(turned, 1)

            def along_w(m, count):
                pe.wait_ge(x1t_ready, count)
                for pair in range(2):
                    for r in range(2):
                        col = (m * GROUP + 2 * pair + r) * MODES
                        for s in range(2):
                            ins = pe.matmul(ps_aw[:, col:col + MODES], x1t[pair][:, 2 * r + s, :],
                                            tab("dw")[:, s * MODES:(s + 1) * MODES],
                                            start=s == 0, stop=s == 1)
                ins.then_inc(w_done, 1)

            def moments(step):
                pe.wait_ge(vec_ready, step)
                pe.matmul(ps_st[:, 0:4], tab("gavg"), vec[:, :, :].rearrange("p m n -> p (m n)"),
                          start=True, stop=True).then_inc(group_sum, 1)

            def mix_mean(step):
                pe.wait_ge(rm_ready, step)
                pe.matmul(ps_st[:, 4:5], mt[:, 0, :], rm[:, 0:1], start=True, stop=True).then_inc(mean_mix, 1)

            pe.wait_ge(mats_ready, 1)
            moments(1)
            mix_mean(1)
            with pe.Fori(0, B) as b:
                g0 = b * GROUPS

                def start_mix():
                    pe.wait_ge(wlh_ready, b + 1)
                    pe.wait_ge(spec_read, 4 * b + 2)

                mix(0, 0, 0, start_mix)
                mix(1, 0, 1, lambda: pe.wait_ge(spec_read, 4 * b + 4))
                turn(0, 0, g0 + 1, lambda pair: pe.wait_ge(awt_ready, 8 * b + 8))
                with pe.Fori(0, PAIRS - 1) as k:
                    for m in range(4):
                        n = g0 + 4 * k + m
                        nx = m + 2
                        mix(nx % 2, 2 * k + nx // 2, nx % 2, lambda: pe.wait_ge(x1_ready, n + 1))
                        if m == 0:
                            pe.wait_ge(aw_ready, 8 * b + k + 8)
                        along_w(m, 2 * n + 2)
                        turn((m + 1) // 2 % 2, (m + 1) % 2, n + 2,
                             lambda pair: pe.wait_ge(x1t_ready, 2 * n + pair + 1))
                for m in range(4):
                    n = g0 + 4 * (PAIRS - 1) + m
                    nx = m + 2
                    if nx < 4:
                        mix(nx % 2, 2 * (PAIRS - 1) + nx // 2, nx % 2, lambda: pe.wait_ge(x1_ready, n + 1))
                    if m == 0:
                        pe.wait_ge(aw_ready, 8 * b + PAIRS - 1 + 8)
                    if m == 3:
                        moments(b + 2)
                    along_w(m, 2 * n + 2)
                    if m < 3:
                        turn((m + 1) // 2 % 2, (m + 1) % 2, n + 2,
                             lambda pair: pe.wait_ge(x1t_ready, 2 * n + pair + 1))
                pe.wait_ge(aw_ready, 8 * b + 16)

                def along_h(q):
                    pe.wait_ge(awt_ready, 8 * b + 8 + q + 1)
                    for j in range(4):
                        l8 = 4 * (q % 2) + j
                        for i in range(2):
                            ins = pe.matmul(ps_mix[q // 2][0:C, l8 * K2:(l8 + 1) * K2],
                                            awt[q % 2][:, j, C * i:C * i + C],
                                            tab("dh")[:, K2 * i:K2 * i + K2], start=i == 0, stop=i == 1)
                    ins.then_inc(h_done, 1)

                for q in range(MODES // 4):
                    if q >= 2:
                        pe.wait_ge(awt_ready, 8 * b + 8 + q - 1)
                    for j in range(4):
                        l = 4 * q + j
                        ins = pe.transpose(ps_t[q % 2][:, j * P:(j + 1) * P],
                                           aw[:, l:l + (HP - 1) * MODES + 1:MODES], tab("ident"))
                    ins.then_inc(aw_turned, 1)
                    if q == 0:
                        mix_mean(b + 2)
                    if q >= 1:
                        along_h(q - 1)
                along_h(MODES // 4 - 1)

        @block.scalar
        def _(act):
            act.sem_inc(aw_ready, 8)
            act.sem_inc(awt_ready, 8)
            act.sem_inc(spec_read, 4)

            def take(par, buf, g, count, wait):
                act.wait_ge(mixed, count)
                wait()
                for s in range(2):
                    ins = act.activation(x1[buf][:, GROUP * g:GROUP * g + GROUP, s, :],
                                         ps_mix[2 * par + s][:, :].rearrange("p (r w) -> p r w", w=WP),
                                         ACT.Identity, bias=bias[:, s:s + 1])
                ins.then_inc(x1_ready, 1)

            def take_turned(count, done):
                for pair in range(2):
                    act.wait_ge(turned, 2 * count - 1 + pair)
                    if pair == 0:
                        act.wait_ge(w_done, done)
                    act.activation(x1t[pair][:, :, :].rearrange("p a q -> p (a q)"), ps_t[pair][:, :],
                                   ACT.Copy).then_inc(x1t_ready, 1)

            def buffer_free(use, buf):
                act.wait_ge(stored[buf], 16 * use + 16)
                act.wait_ge(x1_stats[buf], use + 1)

            act.sem_inc(w_done, 1)
            act.sem_inc(spec_stored, 32)

            with act.Fori(0, B) as b:
                g0 = b * GROUPS
                act.wait_ge(bias_ready, b + 1)
                take(0, 0, 0, g0 + 1, lambda: buffer_free(b * PAIRS, 0))
                take(1, 0, 1, g0 + 2, lambda: None)
                take_turned(g0 + 1, g0 + 1)
                with act.Fori(0, PAIRS - 1) as k:
                    for m in range(4):
                        n = g0 + 4 * k + m
                        nx = m + 2
                        buf = nx // 2 % 2
                        use = b * PAIRS + k + nx // 4

                        def free():
                            if nx % 2 == 0:
                                buffer_free(use, buf)
                        take(nx % 2, buf, nx % 2, n + 3, free)
                        take_turned(n + 2, n + 2)
                        if m == 3:
                            act.wait_ge(w_done, n + 2)
                            act.activation(aw[:, ds(k * 512, 512)], ps_aw[:, :], ACT.Copy).then_inc(aw_ready, 1)
                for m in range(4):
                    n = g0 + 4 * (PAIRS - 1) + m
                    nx = m + 2
                    if nx < 4:
                        def free():
                            if nx % 2 == 0:
                                buffer_free(b * PAIRS + PAIRS - 1, 1)
                        take(nx % 2, nx // 2 % 2, nx % 2, n + 3, free)
                    if m < 3:
                        take_turned(n + 2, n + 2)
                act.wait_ge(w_done, g0 + GROUPS + 1)
                act.activation(aw[:, (PAIRS - 1) * 512:PAIRS * 512], ps_aw[:, :], ACT.Copy).then_inc(aw_ready, 1)
                for q in range(MODES // 4):
                    act.wait_ge(aw_turned, 8 * b + q + 1)
                    if q >= 2:
                        act.wait_ge(h_done, 8 * b + q - 1)
                    act.activation(awt[q % 2][:, :, :].rearrange("p a q -> p (a q)"), ps_t[q % 2][:, :],
                                   ACT.Copy).then_inc(awt_ready, 1)
                act.wait_ge(spec_ready, b + 1)
                for half in range(2):
                    act.dma_start(spec_scr[:, half, :, ds(b, 1), :].rearrange("c o b m -> o c (b m)"),
                                  spec[:, half, :, :].rearrange("o (c l) k -> o c (l k)", l=4)).then_inc(spec_stored, 16)
            act.wait_ge(spec_stored, 32 * B + 32)


def stage_two(nc, weights, spec_scr, f_scr):
    with ExitStack() as ctx:
        def sb(name, shape):
            return ctx.enter_context(nc.sbuf_tensor(name, shape, F32))

        def sem(name):
            return ctx.enter_context(nc.semaphore(name))

        HALF = MODES // 2
        wq = [[sb(f"wq{i}{h}", [P, HALF, 4, C]) for h in range(2)] for i in range(2)]
        sq = [sb(f"sq{i}", [P, 32, 4 * MODES]) for i in range(2)]
        fo = [sb(f"fo{i}", [P, 4, 512]) for i in range(2)]
        ps = [ctx.enter_context(nc.psum_tensor(f"ps_f{i}", [P, 512], F32)) for i in range(8)]
        cleared = [sem(f"sq_cleared{i}") for i in range(2)]
        w_in = [[sem(f"wq_in{i}{h}") for h in range(2)] for i in range(2)]
        s_in = [sem(f"sq_in{i}") for i in range(2)]
        done = sem("modes_done")
        act_read = sem("f_act_read")
        dve_read = sem("f_dve_read")
        f_stored = [sem(f"f_stored{i}") for i in range(2)]
        block = ctx.enter_context(nc.Block())
        TURNS = QUADS // 2

        @block.sync
        def _(sp):
            def load_w(row, par, h):
                sp.dma_start(wq[par][h][:, :, :, :].rearrange("p k l o -> p (k l o)"),
                             weights[row, h, :, :].rearrange("a p m -> p (a m)")).then_inc(w_in[par][h], 16)

            for par in range(2):
                for h in range(2):
                    load_w(ds(par, 1), par, h)
            with sp.Fori(0, TURNS - 1) as kq:
                for par in range(2):
                    for h in range(2):
                        sp.wait_ge(done, 8 * kq + 4 * par + 2 * h + 2)
                        load_w(ds(2 * kq + 2 + par, 1), par, h)

        @block.gpsimd
        def _(pool):
            pool.memset(sq[1][:, :, :], 0.0).then_inc(cleared[1], 1)

        @block.tensor
        def _(pe):
            with pe.Fori(0, TURNS) as kq:
                for par in range(2):
                    pe.wait_ge(s_in[par], 32 * kq + 32)
                    for octet in range(4):
                        if octet % 2 == 0:
                            pe.wait_ge(w_in[par][octet // 2], 16 * kq + 16)
                        pe.wait_ge(act_read if octet < 2 else dve_read, 4 * kq + 2 * par + octet % 2 + 1)
                        for k8 in range(8):
                            for g in range(4):
                                k = 8 * octet + k8
                                ins = pe.matmul(ps[4 * par + octet][32 * g:32 * g + 32, k8 * C:(k8 + 1) * C],
                                                sq[par][:, :, g * MODES + k],
                                                wq[par][octet // 2][:, k % HALF, g, :],
                                                start=True, stop=True)
                        ins.then_inc(done, 1)

        @block.scalar
        def _(act):
            for par in range(2):
                act.sem_inc(f_stored[par], 128)

            def load_s(row, par):
                for half in range(2):
                    act.dma_start(sq[par][C * half:C * half + C, B * half:B * half + B, :],
                                  spec_scr[row, half, :, :, :].rearrange("a o b m -> (a o) b m"))\
                       .then_inc(s_in[par], 16)

            def store(kq, par):
                act.wait_ge(act_read, 4 * kq + 2 * par + 2 + 4)
                act.wait_ge(dve_read, 4 * kq + 2 * par + 2 + 4)
                for g in range(4):
                    for half in range(2):
                        first = 32 * g + B * half
                        l = ds(4 * (2 * kq + par) + g, 1)
                        act.dma_start(f_scr[:, l, half * MODES:(half + 1) * MODES, :]
                                      .rearrange("b l k o -> b (l k o)"),
                                      fo[par][first:first + B, :, :].rearrange("b q m -> b (q m)"))\
                           .then_inc(f_stored[par], 16)

            for par in range(2):
                act.wait_ge(cleared[par], 1)
                load_s(ds(par, 1), par)

            def turn(kq, par, reload):
                act.wait_ge(f_stored[par], 128 * kq + 128)
                for octet in range(2):
                    act.wait_ge(done, 8 * kq + 4 * par + octet + 1)
                    act.activation(fo[par][:, octet, :], ps[4 * par + octet][:, :], ACT.Copy).then_inc(act_read, 1)
                act.wait_ge(done, 8 * kq + 4 * par + 4)
                if reload:
                    load_s(ds(2 * kq + 2 + par, 1), par)
                store(kq, par)

            act.sem_inc(act_read, 4)
            with act.Fori(0, TURNS - 1) as kq:
                for par in range(2):
                    turn(kq, par, True)
            for par in range(2):
                turn(TURNS - 1, par, False)
            for par in range(2):
                act.wait_ge(f_stored[par], 128 * TURNS + 128)

        @block.vector
        def _(dve):
            dve.memset(sq[0][:, :, :], 0.0).then_inc(cleared[0], 1)
            dve.sem_inc(dve_read, 4)
            with dve.Fori(0, TURNS) as kq:
                for par in range(2):
                    dve.wait_ge(f_stored[par], 128 * kq + 128)
                    for octet in (2, 3):
                        dve.wait_ge(done, 8 * kq + 4 * par + octet + 1)
                        dve.tensor_copy(fo[par][:, octet, :], ps[4 * par + octet][:, :]).then_inc(dve_read, 1)


def stage_three(nc, tab, x1_scr, f_scr, out):
    with ExitStack() as ctx:
        def sb(name, shape, dt=F32):
            return ctx.enter_context(nc.sbuf_tensor(name, shape, dt))

        def sem(name):
            return ctx.enter_context(nc.semaphore(name))

        chr_ = sb("chr", [P, 2, 2, HP], F32R)
        cwr = sb("cwr", [K2, 2, W], F32R)
        f = sb("f", [MODES, K2, C])
        fq = [sb(f"fq{i}", [K2, 8, 2, K2], F32R) for i in range(2)]
        gw = [sb(f"gw{i}", [P, 8 * W], F32R) for i in range(2)]
        xt = [sb(f"xt{i}", [P, 8, W]) for i in range(4)]
        ot = [sb(f"ot{i}", [P, 8, 2, WP]) for i in range(4)]
        ps_g = [ctx.enter_context(nc.psum_tensor(f"ps_g{i}", [P, 1024], F32)) for i in range(2)]
        ps_o = [ctx.enter_context(nc.psum_tensor(f"ps_o{i}", [P, 1024], F32)) for i in range(2)]
        consts = sem("consts")
        f_in = sem("f_in")
        top_ready = sem("top_ready")
        fq_ready = sem("fq_ready")
        g_done = sem("g_done")
        g_top = sem("g_top")
        gw_ready = sem("gw_ready")
        h_out = sem("h_out")
        x1_in = [sem(f"x1_in{i}") for i in range(4)]
        added = sem("added")
        even_done = sem("even_done")
        odd_done = sem("odd_done")
        out_stored = [sem(f"out_stored{i}") for i in range(4)]
        block = ctx.enter_context(nc.Block())
        STEPS = B * OCT
        TURNS = STEPS // 2

        @block.sync
        def _(sp):
            for buf in range(4):
                sp.sem_inc(out_stored[buf], 16)

            def load(rows, octet, buf):
                cols = ds((buf % 2 * C + 8 * octet) * W, 8 * W)
                sp.dma_start(xt[buf][:, :, :].rearrange("p o w -> p (o w)"), x1_scr[rows, cols])\
                  .then_inc(x1_in[buf], 16)

            def store(turn, buf):
                sp.wait_ge(even_done, 4 * turn + buf + 1)
                sp.wait_ge(odd_done, 4 * turn + buf + 1)
                sp.dma_start(out[ds(4 * turn + buf, 1), :, :].rearrange("a p m -> p (a m)"),
                             ot[buf][:, :, :, :].rearrange("p o j w -> p (o j w)")).then_inc(out_stored[buf], 16)

            PER = OCT // 2
            for buf in range(4):
                load(ds(0, HP), buf // 2, buf)
            with sp.Fori(0, B - 1) as b:
                with sp.Fori(0, PER - 1) as t:
                    for buf in range(4):
                        store(b * PER + t, buf)
                        load(ds(b * HP, HP), 2 * t + 2 + buf // 2, buf)
                for buf in range(4):
                    store(b * PER + PER - 1, buf)
                    load(ds(b * HP + HP, HP), buf // 2, buf)
            with sp.Fori(0, PER - 1) as t:
                for buf in range(4):
                    store((B - 1) * PER + t, buf)
                    load(ds((B - 1) * HP, HP), 2 * t + 2 + buf // 2, buf)
            for buf in range(4):
                store(B * PER - 1, buf)
            for buf in range(4):
                sp.wait_ge(out_stored[buf], 16 * TURNS + 16)

        @block.tensor
        def _(pe):
            def along_w(step, par):
                pe.wait_ge(fq_ready, step + 1)
                for half in range(2):
                    pe.wait_ge(gw_ready, 2 * step + half + 1)
                    for o in range(4):
                        columns = fq[par][:, 4 * half + o, :, :].rearrange("p a k -> p (a k)")
                        for part in range(2):
                            ins = pe.matmul(ps_g[half][:, o * W:(o + 1) * W], columns, cwr[:, part, :],
                                            start=part == 0, stop=part == 1)
                    ins.then_inc(g_done, 1)

            def along_h(step, par, i):
                for half in range(2):
                    if i == 0:
                        pe.wait_ge(gw_ready, 2 * step + half + 1 + 2)
                    pe.wait_ge(added, 4 * step + 2 * i + half + 1)
                    for bank in range(2):
                        col = half * 1024 + bank * 512
                        for part in range(2):
                            ins = pe.matmul(ps_o[half][:, bank * 512:bank * 512 + 512],
                                            chr_[:, part, i, :], gw[par][:, col:col + 512],
                                            start=part == 0, stop=part == 1)
                    ins.then_inc(h_out, 1)

            pe.wait_ge(consts, 2)
            along_w(0, 0)
            with pe.Fori(0, TURNS - 1) as t:
                for par in range(2):
                    along_h(2 * t + par, par, 0)
                    along_w(2 * t + par + 1, 1 - par)
                    along_h(2 * t + par, par, 1)
            along_h(STEPS - 2, 0, 0)
            along_w(STEPS - 1, 1)
            along_h(STEPS - 2, 0, 1)
            along_h(STEPS - 1, 1, 0)
            along_h(STEPS - 1, 1, 1)

        @block.scalar
        def _(act):
            act.sem_inc(h_out, 8)

            def load_f(row):
                act.dma_start(f[:, :, :], f_scr[row, :, :, :].rearrange("a l k o -> (a l) k o")).then_inc(f_in, 16)

            def pick(octet, par):
                for side in range(2):
                    ins = act.activation(fq[par][0:MODES, :, side, :],
                                         f[:, :, ds(octet * 8, 8)].rearrange("l k o -> l o k"), ACT.Copy)
                ins.then_inc(top_ready, 1)

            def take(step, par):
                act.wait_ge(h_out, 4 * step + 4)
                for half in range(2):
                    act.wait_ge(g_done, 2 * step + half + 1)
                    act.activation(gw[par][:, half * 1024:half * 1024 + 1024], ps_g[half][:, :],
                                   ACT.Copy).then_inc(g_top, 1)

            load_f(ds(0, 1))
            act.activation(cwr[:, :, :].rearrange("p a w -> p (a w)"), tab("cw")[0:K2, :], ACT.Copy).then_inc(consts, 1)
            act.activation(chr_[:, :, :, :].rearrange("p a i r -> p (a i r)"), tab("ch"), ACT.Copy)\
               .then_inc(consts, 1)
            act.wait_ge(f_in, 16)
            pick(0, 0)

            def element(b, following):
                first = b * OCT
                with act.Fori(0, OCT // 2 - 1) as t:
                    pick(2 * t + 1, 1)
                    take(first + 2 * t, 0)
                    pick(2 * t + 2, 0)
                    take(first + 2 * t + 1, 1)
                pick(OCT - 1, 1)
                take(first + OCT - 2, 0)
                if following is not None:
                    act.wait_ge(fq_ready, first + OCT)
                    load_f(following)
                    act.wait_ge(f_in, 16 * b + 32)
                    pick(0, 0)
                take(first + OCT - 1, 1)

            with act.Fori(0, B - 1) as b:
                element(b, ds(b + 1, 1))
            element(B - 1, None)

        @block.vector
        def _(dve):
            dve.sem_inc(added, 2)
            dve.sem_inc(gw_ready, 2)

            def rest(step, par):
                low = slice(K2, P)
                for half in range(2):
                    dve.wait_ge(g_top, 2 * step + half + 1)
                    part = gw[par][low, half * 1024:half * 1024 + 1024]
                    dve.tensor_tensor(part, ps_g[half][low, :], part.bitcast(F32), ALU.subtract).then_inc(gw_ready, 1)

            def unit(t, buf):
                unit = 4 * t + buf
                dve.wait_ge(x1_in[buf], 16 * t + 16)
                for half in range(2):
                    dve.wait_ge(h_out, 2 * unit + half + 1 + 8)
                    part = xt[buf][:, 4 * half:4 * half + 4, :].rearrange("p o w -> p (o w)")
                    dve.tensor_tensor(part, part, ps_o[half][:, :], ALU.add).then_inc(added, 1)
                dve.wait_ge(added, 2 * unit + 2 + 2)
                dve.wait_ge(out_stored[buf], 16 * t + 16)
                dve.tensor_tensor(ot[buf][:, :, 0, :], xt[buf][:, :, 0:WP], xt[buf][:, :, WP:W],
                                  ALU.add).then_inc(even_done, 1)

            rest(0, 0)
            with dve.Fori(0, TURNS - 1) as t:
                unit(t, 0)
                rest(2 * t + 1, 1)
                unit(t, 1)
                unit(t, 2)
                rest(2 * t + 2, 0)
                unit(t, 3)
            unit(TURNS - 1, 0)
            rest(STEPS - 1, 1)
            for buf in range(1, 4):
                unit(TURNS - 1, buf)

        @block.gpsimd
        def _(pool):
            def rest_of_f(step, octet, par):
                pool.wait_ge(top_ready, step + 1)
                for side in range(2):
                    ins = pool.tensor_tensor(fq[par][MODES:K2, :, side, :],
                                             f[:, :, ds(octet * 8, 8)].rearrange("l k o -> l o k"),
                                             fq[par][0:MODES, :, side, :].bitcast(F32), ALU.subtract)
                ins.then_inc(fq_ready, 1)
                pool.wait_ge(fq_ready, step + 1)

            def odd(t, buf):
                pool.wait_ge(added, 2 * (4 * t + buf) + 2 + 2)
                pool.wait_ge(out_stored[buf], 16 * t + 16)
                pool.tensor_tensor(ot[buf][:, :, 1, :], xt[buf][:, :, 0:WP], xt[buf][:, :, WP:W],
                                   ALU.subtract).then_inc(odd_done, 1)

            PER = OCT // 2
            rest_of_f(0, 0, 0)
            rest_of_f(1, 1, 1)

            def turn(t, step, octet):
                for par in range(2):
                    odd(t, 2 * par)
                    if step is not None:
                        pool.wait_ge(odd_done, 4 * t + 2 * par + 1)
                        rest_of_f(step + par, octet + par, par)
                    odd(t, 2 * par + 1)

            with pool.Fori(0, B - 1) as b:
                with pool.Fori(0, PER - 1) as t:
                    turn(b * PER + t, b * OCT + 2 * t + 2, 2 * t + 2)
                turn(b * PER + PER - 1, b * OCT + OCT, 0)
            with pool.Fori(0, PER - 1) as t:
                turn((B - 1) * PER + t, (B - 1) * OCT + 2 * t + 2, 2 * t + 2)
            turn(TURNS - 1, None, None)


def build(nc, x, mix_t, biases, weights, constants, out):
    x1_scr = nc.dram_tensor("x1_scr", (B * HP, HPITCH), F32, kind="Internal").ap()
    spec_scr = nc.dram_tensor("spec_scr", (QUADS, 2, C, B, 4 * MODES), F32, kind="Internal").ap()
    f_scr = nc.dram_tensor("f_scr", (B, MODES, K2, C), F32, kind="Internal").ap()
    with nc.sbuf_tensor("table", [P, TABLE_COLS], F32) as table:
        def tab(name):
            lo, hi = TABLE[name]
            return table[:, lo:hi]

        with nc.semaphore("table_in") as table_in, nc.Block() as block:
            @block.sync
            def _(sp):
                sp.dma_start(table[:, :], constants).then_inc(table_in, 16)
                sp.wait_ge(table_in, 16)
        stage_one(nc, tab, x, mix_t, biases, x1_scr, spec_scr)
        stage_two(nc, weights, spec_scr, f_scr)
        stage_three(nc, tab, x1_scr, f_scr, out)


def kernel(x, L0_conv_w_LL, L0_conv_b_LL, L0_conv_w_LH, L0_conv_b_LH, L0_conv_w_HL, L0_conv_b_HL,
           L0_conv_w_HH, L0_conv_b_HH, L1_conv_weights1, L1_conv_weights2):
    import concourse.bacc as bacc
    from concourse.bass_utils import run_bass_kernel_spmd

    a = np.asarray
    xs = a(x).reshape(B, C, CHUNKS, CHUNK, 2, WP, 2).transpose(0, 2, 4, 1, 3, 6, 5)
    mix = np.stack([a(w).T for w in (L0_conv_w_LL, L0_conv_w_LH, L0_conv_w_HL, L0_conv_w_HH)], axis=1)
    biases = np.stack([a(v) for v in (L0_conv_b_LL, L0_conv_b_LH, L0_conv_b_HL, L0_conv_b_HH)], axis=1)
    ws = np.stack([a(L1_conv_weights1), a(L1_conv_weights2)])
    ws = ws.reshape(2, C, C, 2, MODES // 2, QUADS, 4).transpose(5, 3, 0, 1, 4, 6, 2)
    arrays = {
        "x": np.ascontiguousarray(xs).reshape(B * CHUNKS, P, CHUNK * W),
        "mix_t": np.ascontiguousarray(mix),
        "biases": np.ascontiguousarray(biases),
        "weights": np.ascontiguousarray(ws).reshape(QUADS, 2, P, 2 * MODES * C),
        "constants": table_of_constants(),
    }
    nc = bacc.Bacc("TRN2", target_bir_lowering=False, num_devices=1)
    args = [nc.dram_tensor(name, v.shape, F32, kind="ExternalInput").ap() for name, v in arrays.items()]
    out = nc.dram_tensor("out", (B * OCT * 2, P, 8 * W), F32, kind="ExternalOutput").ap()
    build(nc, *args, out)
    got = run_bass_kernel_spmd(nc, [arrays], core_ids=[0]).results[0]["out"]
    got = got.reshape(B, OCT, 2, HP, 8, 2, WP).transpose(0, 1, 4, 3, 2, 6, 5)
    return np.ascontiguousarray(got).reshape(B, C, H, W)
```

```python
from contextlib import ExitStack

import concourse.bass as bass
from concourse import mybir
import numpy as np

F32 = mybir.dt.float32
F32R = mybir.dt.float32r
ALU = mybir.AluOpType
ACT = mybir.ActivationFunctionType
ds = bass.ds

P = 128
B, C, H, W = 8, 64, 256, 256
MODES = 32
HP, WP = H // 2, W // 2
K2 = 2 * MODES
CHUNK = 8
CHUNKS = HP // CHUNK
PAIRS = CHUNKS // 2
GROUP = 4
GROUPS = HP // GROUP
GCOLS = GROUP * WP
QUADS = MODES // 4
HALF = MODES // 2
SLOTS = PAIRS
EPS = 1e-5
APITCH = GROUPS * P + 128
HPITCH = P * W + 1024
OCT = C // 8

TABLE = {}
_at = 0
for _name, _width in (("ident", P), ("gavg", P), ("half", P), ("dw", 2 * MODES), ("dh", 2 * K2),
                      ("ch", 4 * HP), ("cw", 4 * WP), ("sign", 2), ("eps", 1), ("power", 1)):
    TABLE[_name] = (_at, _at + _width)
    _at += _width
TABLE_COLS = _at


def split(a):
    a = a.astype(np.float32)
    top = ((a.view(np.uint32) + np.uint32(0x800)) & np.uint32(0xFFFFF000)).view(np.float32)
    return top, a - top


def table_of_constants():
    t = np.zeros((P, TABLE_COLS), np.float64)

    def put(name, a, rows=slice(0, P)):
        lo, hi = TABLE[name]
        t[rows, lo:hi] = a.reshape(a.shape[0], -1)

    part = np.arange(P)
    put("ident", np.eye(P))
    group = (part % C) // 2
    put("gavg", (group[:, None] == group[None, :]) / 4.0)
    put("half", 0.5 * np.eye(P))
    rows = np.concatenate([np.arange(MODES), H - MODES + np.arange(MODES)])
    space = np.arange(H)
    cosines = np.cos(np.pi * ((rows[:, None] * space[None, :]) % (2 * (H - 1))) / (H - 1))
    ends_space = np.where((space == 0) | (space == H - 1), 1.0, 2.0)
    ends_rows = np.where((rows == 0) | (rows == H - 1), 1.0, 2.0)
    forward = cosines * ends_space[None, :]
    inverse = cosines * ends_rows[:, None]
    even, odd = forward[:MODES, 0::2], forward[:MODES, 1::2]
    put("dw", np.stack([even + odd, even - odd]).transpose(2, 0, 1))
    order = np.arange(HP).reshape(GROUPS, GROUP).T.reshape(-1)
    put("dh", np.stack([forward[:, 0::2], forward[:, 1::2]])[:, :, order].transpose(2, 0, 1))
    ch = np.stack([inverse[:, 0::2], inverse[:, 1::2]], axis=1)
    put("ch", np.tile(np.stack(split(ch), axis=1), (2, 1, 1, 1)))
    even, odd = inverse[:MODES, 0::2], inverse[:MODES, 1::2]
    cw = np.stack([(even + odd) / 2, (even - odd) / 2], axis=1)
    put("cw", np.tile(np.stack(split(cw), axis=1), (2, 1, 1, 1)), slice(0, 2 * MODES))
    upper = np.where(part < C, 1.0, -1.0)
    put("sign", np.stack([upper, -upper], axis=1))
    put("eps", np.full((P, 1), EPS))
    put("power", np.full((P, 1), -0.5))
    return t.astype(np.float32)


def weights_in(sp, weights, half, lh, w_in):
    cols = HALF * 4 * C
    slot = half % SLOTS
    sp.dma_start(lh[:, slot * cols:(slot + 1) * cols], weights[half, :, :]).then_inc(w_in[slot], 16)


def stage_one(nc, table, constants, tab, x, mix_t, biases, x1_scr, a_scr, spec_scr, lh, weights, w_in):
    with ExitStack() as ctx:
        def sb(name, shape):
            return ctx.enter_context(nc.sbuf_tensor(name, shape, F32))

        def sem(name):
            return ctx.enter_context(nc.semaphore(name))

        raw = [sb(f"raw{i}", [P, CHUNK, 2, WP]) for i in range(2)]
        x1 = [sb(f"x1_{i}", [P, CHUNK, 2, WP]) for i in range(2)]
        x1t = [sb(f"x1t{i}", [P, 4, P]) for i in range(2)]
        aw = sb("aw", [P, 4 * P])
        a = sb("a", [P, MODES, P])
        spec = sb("spec", [P, 2, MODES // 2, MODES])
        wraw = sb("wraw", [P, 4, C])
        mt = sb("mt", [P, 2, P])
        wlh = sb("wlh", [P, 2, P])
        braw = sb("braw", [P, 4])
        bconst = sb("bconst", [P, 2])
        bias = sb("bias", [P, 2])
        st_x = sb("st_x", [P, 2 * GROUPS * 6])
        st_x1 = sb("st_x1", [P, 2, GROUPS * 6])
        agg_x = sb("agg_x", [P, 2])
        agg = sb("agg", [P, 2, 2])
        vec = [sb(f"vec{i}", [P, 2]) for i in range(2)]
        gst = [sb(f"gst{i}", [P, 2]) for i in range(2)]
        sm = [sb(f"sm{i}", [P, 2]) for i in range(2)]
        var = [sb(f"var{i}", [P, 1]) for i in range(2)]
        rstd = [sb(f"rstd{i}", [P, 1]) for i in range(2)]
        rm = sb("rm", [P, 1])
        dc = sb("dc", [P, 1])

        ps_mix = [ctx.enter_context(nc.psum_tensor(f"ps_mix{i}", [P, 512], F32)) for i in range(4)]
        ps_t = [ctx.enter_context(nc.psum_tensor(f"ps_t{i}", [P, 512], F32)) for i in range(2)]
        ps_aw = ctx.enter_context(nc.psum_tensor("ps_aw", [P, 512], F32))
        ps_h = ctx.enter_context(nc.psum_tensor("ps_h", [P, 512], F32))

        sums = [ps_t[0][:, 0:2], ps_h[:, 0:2]]
        mean_term = ps_t[0][:, 2:3]

        x_bufs = raw + x1

        params_in = sem("params_in")
        mats_ready = sem("mats_ready")
        loaded = [sem(f"loaded{i}") for i in range(4)]
        made_dve = sem("made_dve")
        made_pool = sem("made_pool")
        vec_ready = [sem(f"vec_ready{i}") for i in range(2)]
        group_sum = [sem(f"group_sum{i}") for i in range(2)]
        sum_read = [sem(f"sum_read{i}") for i in range(2)]
        var_ready = [sem(f"var_ready{i}") for i in range(2)]
        pow_done = [sem(f"pow_done{i}") for i in range(2)]
        chain = [sem(f"chain{i}") for i in range(2)]
        rm_ready = sem("rm_ready")
        x1_norm = sem("x1_norm")
        mean_mix = sem("mean_mix")
        wlh_ready = sem("wlh_ready")
        bias_ready = sem("bias_ready")
        mixed = sem("mixed")
        x1_ready = sem("x1_ready")
        x_stats = sem("x_stats")
        x1_stats = [sem(f"x1_stats{i}") for i in range(2)]
        stored = [sem(f"stored{i}") for i in range(2)]
        turned = sem("turned")
        x1t_ready = sem("x1t_ready")
        w_done = sem("w_done")
        aw_ready = sem("aw_ready")
        aw_stored = sem("aw_stored")
        a_in = sem("a_in")
        h_done = sem("h_done")
        spec_read = sem("spec_read")
        spec_ready = sem("spec_ready")
        spec_stored = sem("spec_stored")

        def lh_cols(c, g, s, cols=GCOLS):
            return ds(c * (4 * GCOLS) + (g * 2 + s) * GCOLS, cols)

        block = ctx.enter_context(nc.Block())

        @block.sync
        def _(sp):
            for buf in range(2):
                sp.sem_inc(stored[buf], 16)
            sp.sem_inc(spec_stored, 64)

            def load(row, buf):
                sp.dma_start(x_bufs[buf][:, :, :, :].rearrange("p r j w -> p (r j w)"),
                             x[row, :, :].rearrange("a p m -> p (a m)")).then_inc(loaded[buf], 16)

            for buf in range(4):
                load(ds(buf, 1), buf)
            with sp.Fori(1, CHUNKS // 4) as k:
                for buf in range(4):
                    sp.wait_ge(made_dve, 4 * k + buf - 3)
                    sp.wait_ge(made_pool, 4 * k + buf - 3)
                    load(ds(4 * k + buf, 1), buf)

            def store(row, count, buf):
                sp.wait_ge(x1_ready, count)
                sp.dma_start(x1_scr[row, 0:P * W].rearrange("r (p w) -> p r w", w=W),
                             x1[buf][:, :, :, :].rearrange("p r j w -> p r (j w)")).then_inc(stored[buf], 16)

            def load_a(b, at):
                sp.wait_ge(aw_stored, 16 * 8 * b + 16 * 9)
                sp.wait_ge(h_done, 8 * b + 1)
                for row in range(GROUP):
                    part = slice(MODES * row, MODES * (row + 1))
                    sp.dma_start(a[GROUPS * row:GROUPS * (row + 1), :, :],
                                 a_scr[at, part, 0:GROUPS * P].rearrange("b l (g m) -> (b g) l m", m=P))\
                       .then_inc(a_in, 16)

            def pair(b, k, reload, behind=False):
                k = b * PAIRS + k
                if reload:
                    for buf in range(2):
                        sp.wait_ge(made_dve, 2 * k + CHUNKS + buf - 1)
                        sp.wait_ge(made_pool, 2 * k + CHUNKS + buf - 1)
                        load(ds(2 * k + CHUNKS + buf, 1), buf)
                for buf in range(2):
                    store(ds((2 * k + buf) * CHUNK, CHUNK), 4 * k + 2 * buf + 2, buf)
                    if behind and buf == 0:
                        load_a(b - 1, ds(b - 1, 1))

            def store_spectrum(b, at):
                sp.wait_ge(spec_ready, b + 1)
                sp.wait_ge(spec_read, 2 * b + 2 + 1)
                for part in range(2):
                    for half in range(2):
                        sp.dma_start(spec_scr[part * QUADS // 2:(part + 1) * QUADS // 2, half, :, at, :]
                                     .rearrange("c o b m -> o c (b m)"),
                                     spec[C * part:C * part + C, half, :, :].rearrange("o (c l) k -> o c (l k)", l=4))\
                          .then_inc(spec_stored, 16)

            with sp.Fori(0, PAIRS) as k:
                pair(0, k, True)
            pair(1, 0, True, behind=True)
            with sp.Fori(1, PAIRS) as k:
                pair(1, k, True)
            with sp.Fori(2, B - 1) as b:
                pair(b, 0, True, behind=True)
                store_spectrum(b - 2, ds(b - 2, 1))
                with sp.Fori(1, PAIRS) as k:
                    pair(b, k, True)
            LAG = 2

            def spectral_weights(slot):
                sp.wait_ge(mixed, (B - 1) * GROUPS + 4 * slot + 4)
                weights_in(sp, weights, slot, lh, w_in)

            for k in range(PAIRS):
                pair(B - 1, k, False, behind=k == 0)
                if k == 0:
                    store_spectrum(B - 3, ds(B - 3, 1))
                if LAG <= k < PAIRS - 1:
                    spectral_weights(k - LAG)
            store_spectrum(B - 2, ds(B - 2, 1))
            load_a(B - 1, ds(B - 1, 1))
            sp.wait_ge(a_in, 64 * B)
            for slot in range(PAIRS - 1 - LAG, SLOTS):
                spectral_weights(slot)
            store_spectrum(B - 1, ds(B - 1, 1))
            for buf in range(2):
                sp.wait_ge(stored[buf], 16 * (PAIRS * B) + 16)
            sp.wait_ge(spec_stored, 64 * B + 64)

        @block.gpsimd
        def _(pool):
            def high(c, buf, low_too=True):
                v = x_bufs[buf][:, :, :, :]
                if low_too:
                    out = lh[:, lh_cols(c, 1, 0)].rearrange("p (r w) -> p r w", w=WP)
                    pool.tensor_tensor(out, v[:, GROUP:CHUNK, 0, :], v[:, GROUP:CHUNK, 1, :], ALU.add)
                for g in range(2):
                    out = lh[:, lh_cols(c, g, 1)].rearrange("p (r w) -> p r w", w=WP)
                    rows = slice(GROUP * g, GROUP * g + GROUP)
                    ins = pool.tensor_tensor(out, v[:, rows, 0, :], v[:, rows, 1, :], ALU.subtract)
                ins.then_inc(made_pool, 1)

            def power(n, step):
                pool.wait_ge(var_ready[n], step)
                pool.tensor_tensor(rstd[n][:, :], var[n][:, :], tab("power"), ALU.pow).then_inc(pow_done[n], 1)

            with pool.Fori(0, CHUNKS // 4) as k:
                for buf in range(4):
                    pool.wait_ge(loaded[buf], 16 * k + 16)
                    high(4 * k + buf, buf, low_too=buf % 2 == 1)
            power(0, 1)
            with pool.Fori(0, B - 1) as b:
                def next_high(k, buf):
                    pool.wait_ge(mixed, b * GROUPS + 4 * k + 2 * buf + 2)
                    pool.wait_ge(loaded[buf], (b * PAIRS + CHUNKS // 4 + k) * 16 + 16)
                    high(2 * k + buf, buf)

                with pool.Fori(0, PAIRS - 1) as k:
                    for buf in range(2):
                        next_high(k, buf)
                next_high(PAIRS - 1, 0)
                power(0, b + 2)
                next_high(PAIRS - 1, 1)
                power(1, b + 1)
            power(1, B)

        @block.vector
        def _(dve):
            links, base = [0, 0], [None, None]

            def step(n, ins, last=True):
                links[n] += 1
                ins.then_inc(chain[n], 1)
                if last:
                    dve.wait_ge(chain[n], links[n] if base[n] is None else base[n] + links[n])

            for buf in range(2):
                dve.sem_inc(x1_stats[buf], 1)

            def low(c, buf, groups=1):
                v = x_bufs[buf][:, :, :, :]
                for g in range(groups):
                    out = lh[:, lh_cols(c, g, 0)].rearrange("p (r w) -> p r w", w=WP)
                    rows = slice(GROUP * g, GROUP * g + GROUP)
                    ins = dve.tensor_tensor(out, v[:, rows, 0, :], v[:, rows, 1, :], ALU.add)
                ins.then_inc(made_dve, 1)

            def stats_x(c, buf, count):
                dve.wait_ge(loaded[buf], count)
                for g in range(4):
                    ins = dve.bn_stats(st_x[:, ds(c * 24 + g * 6, 6)],
                                       x_bufs[buf][:, 2 * g:2 * g + 2, :, :].rearrange("p r j w -> p (r j w)"))
                ins.then_inc(x_stats, 1)

            def stats_x1(k, buf, count):
                dve.wait_ge(x1_ready, count)
                for g in range(2):
                    for s in range(2):
                        ins = dve.bn_stats(st_x1[:, s, ds(k * 24 + buf * 12 + g * 6, 6)],
                                           x1[buf][:, GROUP * g:GROUP * g + GROUP, s, :])
                ins.then_inc(x1_stats[buf], 1)

            STEPS = (3, 5)

            def moments_x(nth):
                base[0], links[0] = (nth - 1) * STEPS[0] + PROLOGUE, 0
                dve.wait_ge(x_stats, CHUNKS * nth)
                dve.memset(sm[0][:, :], 0.0)
                step(0, dve.bn_aggr(agg_x[:, :], st_x[:, :].rearrange("p (g k) -> p g k", k=6)))
                mean = agg_x[:, 0:1]
                step(0, dve.tensor_copy(vec[0][:, 0:1], mean))
                dve.scalar_tensor_tensor(vec[0][:, 1:2], mean, mean, agg_x[:, 1:2],
                                         ALU.mult, ALU.add).then_inc(vec_ready[0], 1)

            def moments_x1(nth):
                base[1], links[1] = (nth - 1) * STEPS[1], 0
                for buf in range(2):
                    dve.wait_ge(x1_stats[buf], PAIRS * nth + 1)
                dve.memset(sm[1][:, :], 0.0)
                for s in range(2):
                    ins = dve.bn_aggr(agg[:, s, :], st_x1[:, s, :].rearrange("p (g k) -> p g k", k=6))
                step(1, ins)
                for s in range(2):
                    mean = agg[:, 1 - s, 0:1]
                    step(1, dve.scalar_tensor_tensor(sm[1][:, s:s + 1], mean, mean, agg[:, s, 1:2],
                                                     ALU.mult, ALU.add), last=False)
                step(1, dve.tensor_copy(vec[1][:, 0:1], agg[:, 0, 0:1]))
                dve.tensor_tensor(vec[1][:, 1:2], sm[1][:, 0:1], sm[1][:, 1:2], ALU.add).then_inc(vec_ready[1], 1)

            def group_rstd(n, nth):
                dve.wait_ge(group_sum[n], nth)
                dve.tensor_copy(gst[n][:, :], sums[n]).then_inc(sum_read[n], 1)
                dve.wait_ge(sum_read[n], nth)
                step(n, dve.scalar_tensor_tensor(sm[n][:, 0:1], gst[n][:, 0:1], gst[n][:, 0:1],
                                                 tab("eps"), ALU.mult, ALU.subtract))
                dve.tensor_tensor(var[n][:, :], gst[n][:, 1:2], sm[n][:, 0:1], ALU.subtract).then_inc(var_ready[n], 1)
                dve.wait_ge(pow_done[n], nth)

            def mix_weights(nth, used):
                group_rstd(0, nth)
                dve.scalar_tensor_tensor(rm[:, :], rstd[0][:, :], 2.0, gst[0][:, 0:1],
                                         ALU.mult, ALU.mult).then_inc(rm_ready, 1)
                if used is not None:
                    dve.wait_ge(mixed, used)
                for s in range(2):
                    ins = dve.scalar_tensor_tensor(wlh[:, s, :], mt[:, s, :], rstd[0][:, :], tab("half"),
                                                   ALU.mult, ALU.add)
                ins.then_inc(wlh_ready, 1)

            def mix_bias(nth, used):
                if used is not None:
                    dve.wait_ge(x1_ready, used)
                dve.wait_ge(mean_mix, nth)
                dve.tensor_tensor(bias[:, 0:1], bconst[:, 0:1], mean_term, ALU.subtract).then_inc(bias_ready, 1)

            def norm_x1(nth):
                moments_x1(nth)
                group_rstd(1, nth)
                dve.scalar_tensor_tensor(dc[:, :], rstd[1][:, :], float((2 * (H - 1)) * (2 * (W - 1))),
                                         gst[1][:, 0:1], ALU.mult, ALU.mult).then_inc(x1_norm, 1)

            def mean_off(b):
                dve.wait_ge(x1_norm, b + 1)
                dve.wait_ge(spec_read, 2 * b + 1 + 1)
                dve.tensor_scalar(spec[0:C, 0, 0, 0:1], spec[0:C, 0, 0, 0:1], dc[0:C, :], None,
                                  ALU.subtract).then_inc(spec_ready, 1)

            def norm_used(b):
                mean_off(b)
                dve.wait_ge(spec_read, 2 * b + 2 + 1)

            def first_chunk(k, buf):
                stats_x(4 * k + buf, buf, 16 * k + 16)
                low(4 * k + buf, buf, groups=2 - buf % 2)

            def next_stats(b, k, buf):
                stats_x(2 * k + buf, buf, (b * PAIRS + CHUNKS // 4 + k) * 16 + 16)

            def next_low(b, k, buf):
                dve.wait_ge(mixed, b * GROUPS + 4 * k + 2 * buf + 2)
                low(2 * k + buf, buf)

            def this_stats(b, k, buf):
                stats_x1(k, buf, b * GROUPS + 4 * k + 2 * buf + 2)

            def pair(b, k):
                for buf in range(2):
                    next_stats(b, k, buf)
                    next_low(b, k, buf)
                    this_stats(b, k, buf)

            def last_pair(b, behind):
                k = PAIRS - 1
                next_stats(b, k, 0)
                next_low(b, k, 0)
                next_stats(b, k, 1)
                moments_x(b + 2)
                this_stats(b, k, 0)
                mix_weights(b + 2, (b + 1) * GROUPS)
                next_low(b, k, 1)
                mix_bias(b + 2, (b + 1) * GROUPS)
                this_stats(b, k, 1)
                if behind:
                    norm_used(b - 1)
                norm_x1(b + 1)

            for buf in range(4):
                first_chunk(0, buf)
            dve.wait_ge(params_in, 16 * 5)
            for s in range(2):
                lo, hi = wraw[:, 2 * s, :], wraw[:, 2 * s + 1, :]
                for i in range(2):
                    step(0, dve.scalar_tensor_tensor(mt[:, s, C * i:C * i + C], hi, tab("sign")[:, i:i + 1], lo,
                                                     ALU.mult, ALU.add))
                step(0, dve.scalar_tensor_tensor(bconst[:, s:s + 1], braw[:, 2 * s + 1:2 * s + 2],
                                                 tab("sign")[:, 0:1], braw[:, 2 * s:2 * s + 1], ALU.mult, ALU.add))
            step(0, dve.tensor_scalar(mt[:, :, :], mt[:, :, :], 0.25, None, ALU.mult))
            step(0, dve.tensor_scalar(bconst[:, :], bconst[:, :], 0.5, None, ALU.mult))
            step(0, dve.tensor_copy(bias[:, 1:2], bconst[:, 1:2]))
            dve.sem_inc(mats_ready, 1)
            PROLOGUE = links[0]
            with dve.Fori(1, CHUNKS // 4) as k:
                for buf in range(4):
                    first_chunk(k, buf)
            moments_x(1)
            mix_weights(1, None)
            mix_bias(1, None)
            with dve.Fori(0, PAIRS - 1) as k:
                pair(0, k)
            last_pair(0, False)
            with dve.Fori(1, B - 1) as b:
                with dve.Fori(0, PAIRS - 1) as k:
                    pair(b, k)
                last_pair(b, True)
            with dve.Fori(0, PAIRS) as k:
                for buf in range(2):
                    this_stats(B - 1, k, buf)
            norm_used(B - 2)
            norm_x1(B)
            mean_off(B - 1)

        @block.tensor
        def _(pe):
            def mix(g, c, par, wait, made=None):
                wait()
                if made is not None:
                    pe.wait_ge(made_dve, made)
                    pe.wait_ge(made_pool, made)
                for s in range(2):
                    ins = pe.matmul(ps_mix[2 * par + s][:, :], wlh[:, s, :], lh[:, lh_cols(c, g, s)],
                                    start=True, stop=True)
                ins.then_inc(mixed, 1)

            def turn(buf, g, count, wait):
                pe.wait_ge(x1_ready, count)
                for pair in range(2):
                    wait(pair)
                    for r in range(2):
                        for s in range(2):
                            ins = pe.transpose(ps_t[pair][:, (2 * r + s) * P:(2 * r + s + 1) * P],
                                               x1[buf][:, GROUP * g + 2 * pair + r, s, :], tab("ident"))
                    ins.then_inc(turned, 1)

            def along_w(m, count):
                pe.wait_ge(x1t_ready, count)
                for s in range(2):
                    for row in range(GROUP):
                        ins = pe.matmul(ps_aw[MODES * row:MODES * (row + 1), m * P:(m + 1) * P],
                                        tab("dw")[:, s * MODES:(s + 1) * MODES],
                                        x1t[row // 2][:, row % 2 * 2 + s, :], start=s == 0, stop=s == 1)
                ins.then_inc(w_done, 1)

            def moments(n, nth):
                pe.wait_ge(vec_ready[n], nth)
                pe.matmul(sums[n], tab("gavg"), vec[n][:, :],
                          start=True, stop=True).then_inc(group_sum[n], 1)

            def mix_mean(nth):
                pe.wait_ge(rm_ready, nth)
                pe.matmul(mean_term, mt[:, 0, :], rm[:, :], start=True, stop=True).then_inc(mean_mix, 1)

            def along_h(b, q):
                if q == 0:
                    pe.wait_ge(sum_read[1], b + 1)
                    pe.wait_ge(a_in, 64 * b + 64)
                elif q == 4:
                    pe.wait_ge(spec_read, 2 * b + 1 + 1)
                for l in (2 * q, 2 * q + 1):
                    col = l % 8 * K2
                    for i in range(2):
                        for half in range(2):
                            ins = pe.matmul(ps_h[C * half:C * half + C, col:col + K2],
                                            a[:, MODES // 2 * half + l, C * i:C * i + C],
                                            tab("dh")[:, K2 * i:K2 * i + K2], start=i == 0, stop=i == 1)
                ins.then_inc(h_done, 1)

            def element(b, behind, last=False):
                g0 = b * GROUPS

                mix(0, 0, 0, lambda: pe.wait_ge(wlh_ready, b + 1), made=b * CHUNKS + 1)
                mix(1, 0, 1, lambda: None)
                if behind:
                    pe.wait_ge(spec_read, 2 * b - 1)
                    moments(1, b)
                turn(0, 0, g0 + 1, lambda pair: None)

                def quad(k, first=False, h_from=None, more=True):
                    for m in range(4):
                        n = g0 + 4 * k + m
                        nx = m + 2
                        if nx < 4 or more:
                            mix(nx % 2, 2 * k + nx // 2, nx % 2, lambda: pe.wait_ge(x1_ready, n + 1),
                                made=b * CHUNKS + 2 * k + nx // 2 + 1 if nx % 2 == 0 else None)
                        if m == 0 and not (first and not behind):
                            pe.wait_ge(aw_ready, 8 * b + k)
                        if h_from is not None:
                            along_h(b - 1, h_from + m)
                        if m == 3 and not more and not last:
                            pe.wait_ge(x1t_ready, 2 * n + 2)
                            moments(0, b + 2)
                        along_w(m, 2 * n + 2)
                        if m < 3 or more:
                            turn((m + 1) // 2 % 2, (m + 1) % 2, n + 2,
                                 lambda pair: pe.wait_ge(x1t_ready, 2 * n + pair + 1))

                quad(0, first=True)
                if behind:
                    quad(1, h_from=0)
                with pe.Fori(2 if behind else 1, PAIRS - 1) as k:
                    quad(k)
                quad(PAIRS - 1, h_from=4 if behind else None, more=False)
                if not last:
                    mix_mean(b + 2)

            pe.wait_ge(mats_ready, 1)
            moments(0, 1)
            mix_mean(1)
            element(0, False)
            with pe.Fori(1, B - 1) as b:
                element(b, True)
            element(B - 1, True, last=True)
            pe.wait_ge(spec_read, 2 * B - 1)
            moments(1, B)
            for q in range(MODES // 4):
                along_h(B - 1, q)

        @block.scalar
        def _(act):
            act.dma_start(table[:, :], constants).then_inc(params_in, 16)
            for half in range(2):
                act.dma_start(wraw[C * half:C * half + C], mix_t).then_inc(params_in, 16)
                act.dma_start(braw[C * half:C * half + C], biases).then_inc(params_in, 16)
            act.sem_inc(spec_read, 1)
            act.sem_inc(w_done, 1)
            act.sem_inc(h_done, 1)
            act.sem_inc(aw_stored, 16)

            def take(par, buf, g, count, wait):
                act.wait_ge(mixed, count)
                wait()
                for s in range(2):
                    ins = act.activation(x1[buf][:, GROUP * g:GROUP * g + GROUP, s, :],
                                         ps_mix[2 * par + s][:, :].rearrange("p (r w) -> p r w", w=WP),
                                         ACT.Identity, bias=bias[:, s:s + 1])
                ins.then_inc(x1_ready, 1)

            def take_turned(count, done):
                for pair in range(2):
                    act.wait_ge(turned, 2 * count - 1 + pair)
                    if pair == 0:
                        act.wait_ge(w_done, done)
                    act.activation(x1t[pair][:, :, :].rearrange("p a q -> p (a q)"), ps_t[pair][:, :],
                                   ACT.Copy).then_inc(x1t_ready, 1)

            def buffer_free(use, buf):
                act.wait_ge(stored[buf], 16 * use + 16)
                act.wait_ge(x1_stats[buf], use + 1)

            def bank(b, j):
                if j == 0:
                    act.wait_ge(x1_norm, b + 1)
                    act.wait_ge(spec_stored, 64 * b + 64)
                act.wait_ge(h_done, 8 * b + 4 * j + 4 + 1)
                out = spec[:, :, 8 * j:8 * j + 8, :].rearrange("o h l k -> o l h k")
                act.activation(out, ps_h[:, :].rearrange("o (l h k) -> o l h k", l=8, h=2),
                               ACT.Copy, scale=rstd[1][:, :]).then_inc(spec_read, 1)

            def element(b, behind):
                g0 = b * GROUPS
                act.wait_ge(bias_ready, b + 1)
                take(0, 0, 0, g0 + 1, lambda: buffer_free(b * PAIRS, 0))
                take(1, 0, 1, g0 + 2, lambda: None)
                take_turned(g0 + 1, g0 + 1)

                def quad(k, first=False, h_from=None, more=True):
                    for m in range(4):
                        n = g0 + 4 * k + m
                        nx = m + 2
                        buf = nx // 2 % 2
                        use = b * PAIRS + k + nx // 4

                        def free():
                            if nx % 2 == 0:
                                buffer_free(use, buf)
                        if nx < 4 or more:
                            take(nx % 2, buf, nx % 2, n + 3, free)
                        if h_from is not None and m == 3:
                            bank(b - 1, h_from // 4)
                        if m == 3:
                            act.wait_ge(w_done, n + 2)
                            act.wait_ge(aw_stored, 16 * (8 * b + k) + 16)
                            act.activation(aw[:, :], ps_aw[:, :], ACT.Copy).then_inc(aw_ready, 1)
                        if m < 3 or more:
                            take_turned(n + 2, n + 2)
                        if m == 3:
                            act.wait_ge(aw_ready, 8 * b + k + 1)
                            act.dma_start(a_scr[ds(b, 1), :, ds(k * 4 * P, 4 * P)].rearrange("b p m -> (b p) m"),
                                          aw[:, :]).then_inc(aw_stored, 16)

                quad(0, first=True)
                if behind:
                    quad(1, h_from=0)
                with act.Fori(2 if behind else 1, PAIRS - 1) as k:
                    quad(k)
                quad(PAIRS - 1, h_from=4 if behind else None, more=False)

            act.wait_ge(made_dve, CHUNKS)
            act.wait_ge(made_pool, CHUNKS)
            element(0, False)
            with act.Fori(1, B) as b:
                element(b, True)
            for j in range(2):
                bank(B - 1, j)


def stage_two(nc, weights, spec_scr, f_scr, lh, w_in):
    with ExitStack() as ctx:
        def sb(name, shape):
            return ctx.enter_context(nc.sbuf_tensor(name, shape, F32))

        def sem(name):
            return ctx.enter_context(nc.semaphore(name))

        ROUND = SLOTS // 2
        wq = lh[:, :].rearrange("p (s k l o) -> p s k l o", s=SLOTS, k=HALF, l=4)
        sq = [sb(f"sq{i}", [P, 2 * B, 4 * MODES]) for i in range(ROUND)]
        fo = [sb(f"fo{i}", [P, 4, 512]) for i in range(2)]
        ps = [ctx.enter_context(nc.psum_tensor(f"ps_f{i}", [P, 512], F32)) for i in range(8)]
        sq_cleared = sem("sq_cleared")
        ps_cleared = sem("ps_cleared")
        s_in = [sem(f"sq_in{i}") for i in range(ROUND)]
        done = sem("modes_done")
        act_read = sem("f_act_read")
        dve_read = sem("f_dve_read")
        f_stored = [sem(f"f_stored{i}") for i in range(2)]
        block = ctx.enter_context(nc.Block())
        TURNS = QUADS // 2

        @block.sync
        def _(sp):
            for half in range(SLOTS, 2 * QUADS):
                sp.wait_ge(done, 2 * (half - SLOTS) + 2)
                weights_in(sp, weights, half, lh, w_in)

        @block.gpsimd
        def _(pool):
            for buf in range(ROUND):
                pool.memset(sq[buf][0:C, B:2 * B, :], 0.0).then_inc(sq_cleared, 1)
                pool.memset(sq[buf][C:P, 0:B, :], 0.0).then_inc(sq_cleared, 1)

        @block.tensor
        def _(pe):
            pe.wait_ge(ps_cleared, 8)
            with pe.Fori(0, QUADS // ROUND) as r:
                for c in range(ROUND):
                    par = c % 2
                    pe.wait_ge(s_in[c], 32 * r + 32)
                    pe.wait_ge(sq_cleared, 2 * c + 2)
                    for octet in range(4):
                        slot = 2 * c + octet // 2
                        if octet % 2 == 0:
                            pe.wait_ge(w_in[slot], 16 * r + 16)
                        pe.wait_ge(act_read if octet < 2 else dve_read, 2 * (r * ROUND + c) + octet % 2 + 1)
                        for k8 in range(8):
                            for g in range(4):
                                k = 8 * octet + k8
                                ins = pe.matmul(ps[4 * par + octet][32 * g:32 * g + 2 * B, k8 * C:(k8 + 1) * C],
                                                sq[c][:, :, g * MODES + k], wq[:, slot, k % HALF, g, :],
                                                start=True, stop=True)
                        ins.then_inc(done, 1)

        @block.scalar
        def _(act):
            for par in range(2):
                act.sem_inc(f_stored[par], 128)

            def load_s(chunk):
                buf = chunk % ROUND
                for half in range(2):
                    act.dma_start(sq[buf][C * half:C * half + C, B * half:B * half + B, :],
                                  spec_scr[chunk, half, :, :, :]).then_inc(s_in[buf], 16)

            def store(kq, par):
                act.wait_ge(act_read, 4 * kq + 2 * par + 2 + 4)
                act.wait_ge(dve_read, 4 * kq + 2 * par + 2 + 4)
                for g in range(4):
                    for half in range(2):
                        first = 32 * g + B * half
                        l = ds(4 * (2 * kq + par) + g, 1)
                        act.dma_start(f_scr[:, l, half * MODES:(half + 1) * MODES, :]
                                      .rearrange("b l k o -> b (l k o)"),
                                      fo[par][first:first + B, :, :].rearrange("b q m -> b (q m)"))\
                           .then_inc(f_stored[par], 16)

            for chunk in range(ROUND):
                load_s(chunk)
            act.sem_inc(act_read, 4)
            for chunk in range(QUADS):
                kq, par = chunk // 2, chunk % 2
                act.wait_ge(f_stored[par], 128 * kq + 128)
                for octet in range(2):
                    act.wait_ge(done, 4 * chunk + octet + 1)
                    act.activation(fo[par][:, octet, :], ps[4 * par + octet][:, :], ACT.Copy).then_inc(act_read, 1)
                if chunk + ROUND < QUADS:
                    act.wait_ge(done, 4 * chunk + 4)
                    load_s(chunk + ROUND)
                store(kq, par)
            for par in range(2):
                act.wait_ge(f_stored[par], 128 * TURNS + 128)

        @block.vector
        def _(dve):
            for bank in range(8):
                dve.memset(ps[bank][:, :], 0.0).then_inc(ps_cleared, 1)
            dve.sem_inc(dve_read, 4)
            with dve.Fori(0, TURNS) as kq:
                for par in range(2):
                    dve.wait_ge(f_stored[par], 128 * kq + 128)
                    for octet in (2, 3):
                        dve.wait_ge(done, 8 * kq + 4 * par + octet + 1)
                        dve.tensor_copy(fo[par][:, octet, :], ps[4 * par + octet][:, :]).then_inc(dve_read, 1)


def stage_three(nc, tab, x1_scr, f_scr, out):
    with ExitStack() as ctx:
        def sb(name, shape, dt=F32):
            return ctx.enter_context(nc.sbuf_tensor(name, shape, dt))

        def sem(name):
            return ctx.enter_context(nc.semaphore(name))

        chr_ = sb("chr", [P, 2, 2, HP], F32R)
        cwr = sb("cwr", [K2, 2, W], F32R)
        f = sb("f", [MODES, K2, C])
        fq = [sb(f"fq{i}", [K2, 8, 2, K2], F32R) for i in range(2)]
        gw = [sb(f"gw{i}", [P, 8 * W], F32R) for i in range(2)]
        xt = [sb(f"xt{i}", [P, 8, W]) for i in range(4)]
        ot = [sb(f"ot{i}", [P, 8, 2, WP]) for i in range(4)]
        ps_g = [ctx.enter_context(nc.psum_tensor(f"ps_g{i}", [P, 1024], F32)) for i in range(2)]
        ps_o = [ctx.enter_context(nc.psum_tensor(f"ps_o{i}", [P, 1024], F32)) for i in range(2)]
        consts = sem("consts")
        f_in = sem("f_in")
        top_ready = sem("top_ready")
        fq_ready = sem("fq_ready")
        g_done = sem("g_done")
        g_top = sem("g_top")
        gw_ready = sem("gw_ready")
        h_out = sem("h_out")
        x1_in = [sem(f"x1_in{i}") for i in range(4)]
        added = sem("added")
        even_done = sem("even_done")
        odd_done = sem("odd_done")
        out_stored = [sem(f"out_stored{i}") for i in range(4)]
        block = ctx.enter_context(nc.Block())
        STEPS = B * OCT
        TURNS = STEPS // 2

        @block.sync
        def _(sp):
            for buf in range(4):
                sp.sem_inc(out_stored[buf], 16)

            def load(rows, octet, buf):
                cols = ds((buf % 2 * C + 8 * octet) * W, 8 * W)
                sp.dma_start(xt[buf][:, :, :].rearrange("p o w -> p (o w)"), x1_scr[rows, cols])\
                  .then_inc(x1_in[buf], 16)

            def store(turn, buf):
                sp.wait_ge(even_done, 4 * turn + buf + 1)
                sp.wait_ge(odd_done, 4 * turn + buf + 1)
                sp.dma_start(out[ds(4 * turn + buf, 1), :, :].rearrange("a p m -> p (a m)"),
                             ot[buf][:, :, :, :].rearrange("p o j w -> p (o j w)")).then_inc(out_stored[buf], 16)

            PER = OCT // 2
            for buf in range(4):
                load(ds(0, HP), buf // 2, buf)
            with sp.Fori(0, B - 1) as b:
                with sp.Fori(0, PER - 1) as t:
                    for buf in range(4):
                        store(b * PER + t, buf)
                        load(ds(b * HP, HP), 2 * t + 2 + buf // 2, buf)
                for buf in range(4):
                    store(b * PER + PER - 1, buf)
                    load(ds(b * HP + HP, HP), buf // 2, buf)
            with sp.Fori(0, PER - 1) as t:
                for buf in range(4):
                    store((B - 1) * PER + t, buf)
                    load(ds((B - 1) * HP, HP), 2 * t + 2 + buf // 2, buf)
            for buf in range(4):
                store(B * PER - 1, buf)
            for buf in range(4):
                sp.wait_ge(out_stored[buf], 16 * TURNS + 16)

        @block.tensor
        def _(pe):
            def along_w(step, par):
                pe.wait_ge(fq_ready, step + 1)
                for half in range(2):
                    pe.wait_ge(gw_ready, 2 * step + half + 1)
                    for o in range(4):
                        columns = fq[par][:, 4 * half + o, :, :].rearrange("p a k -> p (a k)")
                        for part in range(2):
                            ins = pe.matmul(ps_g[half][:, o * W:(o + 1) * W], columns, cwr[:, part, :],
                                            start=part == 0, stop=part == 1)
                    ins.then_inc(g_done, 1)

            def along_h(step, par, i):
                for half in range(2):
                    if i == 0:
                        pe.wait_ge(gw_ready, 2 * step + half + 1 + 2)
                    pe.wait_ge(added, 4 * step + 2 * i + half + 1)
                    for bank in range(2):
                        col = half * 1024 + bank * 512
                        for part in range(2):
                            ins = pe.matmul(ps_o[half][:, bank * 512:bank * 512 + 512],
                                            chr_[:, part, i, :], gw[par][:, col:col + 512],
                                            start=part == 0, stop=part == 1)
                    ins.then_inc(h_out, 1)

            pe.wait_ge(consts, 2)
            along_w(0, 0)
            with pe.Fori(0, TURNS - 1) as t:
                for par in range(2):
                    along_h(2 * t + par, par, 0)
                    along_w(2 * t + par + 1, 1 - par)
                    along_h(2 * t + par, par, 1)
            along_h(STEPS - 2, 0, 0)
            along_w(STEPS - 1, 1)
            along_h(STEPS - 2, 0, 1)
            along_h(STEPS - 1, 1, 0)
            along_h(STEPS - 1, 1, 1)

        @block.scalar
        def _(act):
            act.sem_inc(h_out, 8)

            def load_f(row):
                act.dma_start(f[:, :, :], f_scr[row, :, :, :].rearrange("a l k o -> (a l) k o")).then_inc(f_in, 16)

            def pick(octet, par):
                for side in range(2):
                    ins = act.activation(fq[par][0:MODES, :, side, :],
                                         f[:, :, ds(octet * 8, 8)].rearrange("l k o -> l o k"), ACT.Copy)
                ins.then_inc(top_ready, 1)

            def take(step, par):
                act.wait_ge(h_out, 4 * step + 4)
                for half in range(2):
                    act.wait_ge(g_done, 2 * step + half + 1)
                    act.activation(gw[par][:, half * 1024:half * 1024 + 1024], ps_g[half][:, :],
                                   ACT.Copy).then_inc(g_top, 1)

            load_f(ds(0, 1))
            act.activation(cwr[:, :, :].rearrange("p a w -> p (a w)"), tab("cw")[0:K2, :], ACT.Copy).then_inc(consts, 1)
            act.activation(chr_[:, :, :, :].rearrange("p a i r -> p (a i r)"), tab("ch"), ACT.Copy)\
               .then_inc(consts, 1)
            act.wait_ge(f_in, 16)
            pick(0, 0)

            def element(b, following):
                first = b * OCT
                with act.Fori(0, OCT // 2 - 1) as t:
                    pick(2 * t + 1, 1)
                    take(first + 2 * t, 0)
                    pick(2 * t + 2, 0)
                    take(first + 2 * t + 1, 1)
                pick(OCT - 1, 1)
                take(first + OCT - 2, 0)
                if following is not None:
                    act.wait_ge(fq_ready, first + OCT)
                    load_f(following)
                    act.wait_ge(f_in, 16 * b + 32)
                    pick(0, 0)
                take(first + OCT - 1, 1)

            with act.Fori(0, B - 1) as b:
                element(b, ds(b + 1, 1))
            element(B - 1, None)

        @block.vector
        def _(dve):
            dve.sem_inc(added, 2)
            dve.sem_inc(gw_ready, 2)

            def rest(step, par):
                low = slice(K2, P)
                for half in range(2):
                    dve.wait_ge(g_top, 2 * step + half + 1)
                    part = gw[par][low, half * 1024:half * 1024 + 1024]
                    dve.tensor_tensor(part, ps_g[half][low, :], part.bitcast(F32), ALU.subtract).then_inc(gw_ready, 1)

            def unit(t, buf):
                unit = 4 * t + buf
                dve.wait_ge(x1_in[buf], 16 * t + 16)
                for half in range(2):
                    dve.wait_ge(h_out, 2 * unit + half + 1 + 8)
                    part = xt[buf][:, 4 * half:4 * half + 4, :].rearrange("p o w -> p (o w)")
                    dve.tensor_tensor(part, part, ps_o[half][:, :], ALU.add).then_inc(added, 1)
                dve.wait_ge(added, 2 * unit + 2 + 2)
                dve.wait_ge(out_stored[buf], 16 * t + 16)
                dve.tensor_tensor(ot[buf][:, :, 0, :], xt[buf][:, :, 0:WP], xt[buf][:, :, WP:W],
                                  ALU.add).then_inc(even_done, 1)

            rest(0, 0)
            with dve.Fori(0, TURNS - 1) as t:
                unit(t, 0)
                rest(2 * t + 1, 1)
                unit(t, 1)
                unit(t, 2)
                rest(2 * t + 2, 0)
                unit(t, 3)
            unit(TURNS - 1, 0)
            rest(STEPS - 1, 1)
            for buf in range(1, 4):
                unit(TURNS - 1, buf)

        @block.gpsimd
        def _(pool):
            def rest_of_f(step, octet, par):
                pool.wait_ge(top_ready, step + 1)
                for side in range(2):
                    ins = pool.tensor_tensor(fq[par][MODES:K2, :, side, :],
                                             f[:, :, ds(octet * 8, 8)].rearrange("l k o -> l o k"),
                                             fq[par][0:MODES, :, side, :].bitcast(F32), ALU.subtract)
                ins.then_inc(fq_ready, 1)
                pool.wait_ge(fq_ready, step + 1)

            def odd(t, buf):
                pool.wait_ge(added, 2 * (4 * t + buf) + 2 + 2)
                pool.wait_ge(out_stored[buf], 16 * t + 16)
                pool.tensor_tensor(ot[buf][:, :, 1, :], xt[buf][:, :, 0:WP], xt[buf][:, :, WP:W],
                                   ALU.subtract).then_inc(odd_done, 1)

            PER = OCT // 2
            rest_of_f(0, 0, 0)
            rest_of_f(1, 1, 1)

            def turn(t, step, octet):
                for par in range(2):
                    odd(t, 2 * par)
                    if step is not None:
                        pool.wait_ge(odd_done, 4 * t + 2 * par + 1)
                        rest_of_f(step + par, octet + par, par)
                    odd(t, 2 * par + 1)

            with pool.Fori(0, B - 1) as b:
                with pool.Fori(0, PER - 1) as t:
                    turn(b * PER + t, b * OCT + 2 * t + 2, 2 * t + 2)
                turn(b * PER + PER - 1, b * OCT + OCT, 0)
            with pool.Fori(0, PER - 1) as t:
                turn((B - 1) * PER + t, (B - 1) * OCT + 2 * t + 2, 2 * t + 2)
            turn(TURNS - 1, None, None)


def build(nc, x, mix_t, biases, weights, constants, out):
    x1_scr = nc.dram_tensor("x1_scr", (B * HP, HPITCH), F32, kind="Internal").ap()
    a_scr = nc.dram_tensor("a_scr", (B, P, APITCH), F32, kind="Internal").ap()
    spec_scr = nc.dram_tensor("spec_scr", (QUADS, 2, C, B, 4 * MODES), F32, kind="Internal").ap()
    f_scr = nc.dram_tensor("f_scr", (B, MODES, K2, C), F32, kind="Internal").ap()
    with nc.sbuf_tensor("table", [P, TABLE_COLS], F32) as table:
        def tab(name):
            lo, hi = TABLE[name]
            return table[:, lo:hi]

        with ExitStack() as ctx:
            lh = ctx.enter_context(nc.sbuf_tensor("lh", [P, CHUNKS * 2 * 2 * GCOLS], F32))
            w_in = [ctx.enter_context(nc.semaphore(f"w_in{i}")) for i in range(SLOTS)]
            stage_one(nc, table, constants, tab, x, mix_t, biases, x1_scr, a_scr, spec_scr, lh, weights, w_in)
            stage_two(nc, weights, spec_scr, f_scr, lh, w_in)
        stage_three(nc, tab, x1_scr, f_scr, out)


def kernel(x, L0_conv_w_LL, L0_conv_b_LL, L0_conv_w_LH, L0_conv_b_LH, L0_conv_w_HL, L0_conv_b_HL,
           L0_conv_w_HH, L0_conv_b_HH, L1_conv_weights1, L1_conv_weights2):
    import concourse.bacc as bacc
    from concourse.bass_utils import run_bass_kernel_spmd

    a = np.asarray
    xs = a(x).reshape(B, C, CHUNKS, CHUNK, 2, WP, 2).transpose(0, 2, 4, 1, 3, 6, 5)
    mix = np.stack([a(w).T for w in (L0_conv_w_LL, L0_conv_w_LH, L0_conv_w_HL, L0_conv_w_HH)], axis=1)
    biases = np.stack([a(v) for v in (L0_conv_b_LL, L0_conv_b_LH, L0_conv_b_HL, L0_conv_b_HH)], axis=1)
    ws = np.stack([a(L1_conv_weights1), a(L1_conv_weights2)])
    ws = ws.reshape(2, C, C, 2, MODES // 2, QUADS, 4).transpose(5, 3, 0, 1, 4, 6, 2)
    arrays = {
        "x": np.ascontiguousarray(xs).reshape(B * CHUNKS, P, CHUNK * W),
        "mix_t": np.ascontiguousarray(mix),
        "biases": np.ascontiguousarray(biases),
        "weights": np.ascontiguousarray(ws).reshape(2 * QUADS, P, 4 * HALF * C),
        "constants": table_of_constants(),
    }
    nc = bacc.Bacc("TRN2", target_bir_lowering=False, num_devices=1)
    args = [nc.dram_tensor(name, v.shape, F32, kind="ExternalInput").ap() for name, v in arrays.items()]
    out = nc.dram_tensor("out", (B * OCT * 2, P, 8 * W), F32, kind="ExternalOutput").ap()
    build(nc, *args, out)
    got = run_bass_kernel_spmd(nc, [arrays], core_ids=[0]).results[0]["out"]
    got = got.reshape(B, OCT, 2, HP, 8, 2, WP).transpose(0, 1, 4, 3, 2, 6, 5)
    return np.ascontiguousarray(got).reshape(B, C, H, W)
```
